# Optimizing a Trainium2 kernel written in Bass

```python
import numpy as np
import jax
import jax.numpy as jnp

def _softmax(x, axis=-1):
    return jax.nn.softmax(x, axis=axis)

def _gelu(x):
    return jax.nn.gelu(x, approximate=True)

def _silu(x):
    return jax.nn.silu(x)

def _sigmoid(x):
    return jax.nn.sigmoid(x)

def _layernorm(x, axis=-1, eps=1e-05):
    m = jnp.mean(x, axis=axis, keepdims=True)
    v = jnp.var(x, axis=axis, keepdims=True)
    return (x - m) / jnp.sqrt(v + eps)

def _scatter_add(tgt, idx, src, axis=0):
    return tgt.at[idx].add(src)

def _segment_sum(src, seg, n):
    return jax.ops.segment_sum(src, seg, n)
kernel_name = 'mk_adaln_d1_jaxref_r4_6a21e9'

def setup_inputs(seed: int=0):
    np.random.seed(seed)
    _w = jnp.asarray

    def _L0_attn_setup():
        import jax, jax.numpy as jnp
        import numpy as np
        H = 16
        D = 256

        def _split_heads(t):
            b, s, _ = t.shape
            return t.reshape(b, s, H, D // H).transpose(0, 2, 1, 3)
        key = jax.random.key(seed)
        ks = jax.random.split(key, 9)
        s = 1.0 / np.sqrt(D).astype(np.float32)
        return {'x': jax.random.normal(ks[0], (2, 512, D), dtype=jnp.float32), 'wq': jax.random.normal(ks[1], (D, D), dtype=jnp.float32) * s, 'bq': jax.random.normal(ks[2], (D,), dtype=jnp.float32) * s, 'wk': jax.random.normal(ks[3], (D, D), dtype=jnp.float32) * s, 'bk': jax.random.normal(ks[4], (D,), dtype=jnp.float32) * s, 'wv': jax.random.normal(ks[5], (D, D), dtype=jnp.float32) * s, 'bv': jax.random.normal(ks[6], (D,), dtype=jnp.float32) * s, 'wo': jax.random.normal(ks[7], (D, D), dtype=jnp.float32) * s, 'bo': jax.random.normal(ks[8], (D,), dtype=jnp.float32) * s}
    _L0_attn_in = _L0_attn_setup()

    def _L0_ffn_setup():
        import jax, jax.numpy as jnp
        import numpy as np
        H_DIM, E_DIM = (256, 128)
        N_SHARED, N_ROUTED, TOP_K = (2, 16, 4)
        B, S = (4, 512)
        key = jax.random.key(seed)
        ks = jax.random.split(key, 6)
        sc = 1.0 / np.sqrt(H_DIM)
        ec = 1.0 / np.sqrt(E_DIM)
        return {'x': jax.random.normal(ks[0], (B, S, H_DIM), dtype=jnp.float32), 'shared_up': jax.random.uniform(ks[1], (N_SHARED, E_DIM, H_DIM), jnp.float32, -sc, sc), 'shared_down': jax.random.uniform(ks[2], (N_SHARED, H_DIM, E_DIM), jnp.float32, -ec, ec), 'routed_up': jax.random.uniform(ks[3], (N_ROUTED, E_DIM, H_DIM), jnp.float32, -sc, sc), 'routed_down': jax.random.uniform(ks[4], (N_ROUTED, H_DIM, E_DIM), jnp.float32, -ec, ec), 'router_w': jax.random.uniform(ks[5], (N_ROUTED, H_DIM), jnp.float32, -sc, sc)}
    _L0_ffn_in = _L0_ffn_setup()
    _L0_c = _w((lambda *s: np.random.randn(*s).astype(np.float32) * 0.05)(8, 256))
    _L0_wmod = _w((lambda *s: np.random.randn(*s).astype(np.float32) * 0.05)(256, 6 * 256) * 256 ** (-0.5))
    _d = {'L0_attn_x': _L0_attn_in['x'], 'L0_attn_wq': _L0_attn_in['wq'], 'L0_attn_bq': _L0_attn_in['bq'], 'L0_attn_wk': _L0_attn_in['wk'], 'L0_attn_bk': _L0_attn_in['bk'], 'L0_attn_wv': _L0_attn_in['wv'], 'L0_attn_bv': _L0_attn_in['bv'], 'L0_attn_wo': _L0_attn_in['wo'], 'L0_attn_bo': _L0_attn_in['bo'], 'L0_ffn_shared_up': _L0_ffn_in['shared_up'], 'L0_ffn_shared_down': _L0_ffn_in['shared_down'], 'L0_ffn_routed_up': _L0_ffn_in['routed_up'], 'L0_ffn_routed_down': _L0_ffn_in['routed_down'], 'L0_ffn_router_w': _L0_ffn_in['router_w'], 'L0_c': _L0_c, 'L0_wmod': _L0_wmod}
    _x0 = _d['L0_attn_x']
    _d['L0_attn_x'] = jax.random.normal(jax.random.fold_in(jax.random.key(seed), 1), (8, 512, 256), dtype=_x0.dtype)
    del _x0
    return _d

def reference(L0_attn_x, L0_attn_wq, L0_attn_bq, L0_attn_wk, L0_attn_bk, L0_attn_wv, L0_attn_bv, L0_attn_wo, L0_attn_bo, L0_ffn_shared_up, L0_ffn_shared_down, L0_ffn_routed_up, L0_ffn_routed_down, L0_ffn_router_w, L0_c, L0_wmod):

    def _L0_attn_ref(x, wq, bq, wk, bk, wv, bv, wo, bo):
        import jax, jax.numpy as jnp
        import numpy as np
        H = 16
        D = 256

        def _split_heads(t):
            b, s, _ = t.shape
            return t.reshape(b, s, H, D // H).transpose(0, 2, 1, 3)
        q = _split_heads(x @ wq + bq)
        k = _split_heads(x @ wk + bk)
        v = _split_heads(x @ wv + bv)
        scale = 1.0 / jnp.sqrt(jnp.asarray(q.shape[-1], q.dtype))
        attn = jnp.einsum('bhqd,bhkd->bhqk', q, k) * scale
        attn = jax.nn.softmax(attn, axis=-1)
        o = jnp.einsum('bhqk,bhkd->bhqd', attn, v)
        b, h, s, d = o.shape
        o = o.transpose(0, 2, 1, 3).reshape(b, s, h * d)
        return o @ wo + bo

    def _L0_ffn_ref(x, shared_up, shared_down, routed_up, routed_down, router_w):
        import jax, jax.numpy as jnp
        import numpy as np
        H_DIM, E_DIM = (256, 128)
        N_SHARED, N_ROUTED, TOP_K = (2, 16, 4)
        B, S = (4, 512)
        b, s, h = x.shape
        xt = x.reshape(-1, h)
        up_s = jnp.einsum('th,seh->tse', xt, shared_up)
        shared = jnp.einsum('tse,she->th', jax.nn.gelu(up_s, approximate=False), shared_down)
        probs = jax.nn.softmax(xt @ router_w.T, axis=-1)
        topk_p, topk_i = jax.lax.top_k(probs, TOP_K)
        gate = jnp.zeros_like(probs).at[jnp.arange(xt.shape[0])[:, None], topk_i].add(topk_p)
        up_r = jnp.einsum('th,reh->tre', xt, routed_up)
        act = jax.nn.gelu(up_r, approximate=False) * gate[:, :, None]
        routed = jnp.einsum('tre,rhe->th', act, routed_down)
        return (shared + routed).reshape(b, s, h)
    x = L0_attn_x
    mod = (_silu(L0_c) @ L0_wmod).reshape(L0_c.shape[0], 6, 1, -1)
    sa, ca, ga, sb, cb, gb = (mod[:, 0], mod[:, 1], mod[:, 2], mod[:, 3], mod[:, 4], mod[:, 5])
    ga = (2 * (ga >= 0) - 1) * jnp.maximum(jnp.abs(ga), 0.25)
    gb = (2 * (gb >= 0) - 1) * jnp.maximum(jnp.abs(gb), 0.25)
    h = _layernorm(x, axis=-1) * (1 + ca) + sa
    x = x + ga * _L0_attn_ref(h, L0_attn_wq, L0_attn_bq, L0_attn_wk, L0_attn_bk, L0_attn_wv, L0_attn_bv, L0_attn_wo, L0_attn_bo)
    h = _layernorm(x, axis=-1) * (1 + cb) + sb
    x = x + gb * _L0_ffn_ref(h, L0_ffn_shared_up, L0_ffn_shared_down, L0_ffn_routed_up, L0_ffn_routed_down, L0_ffn_router_w)
    return x

_drawn_inputs = setup_inputs


def setup_inputs(seed=0):
    import zlib

    import numpy as np

    out = dict(_drawn_inputs(seed))
    spreads = {}
    factors = {'L0_attn_bq': 21.761,
     'L0_attn_bk': 64.0,
     'L0_attn_bv': 3.455,
     'L0_attn_bo': 3.776,
     'L0_ffn_routed_up': 5.216,
     'L0_ffn_routed_down': 4.897,
     'L0_ffn_router_w': 5.544}
    for name, (base, spread) in spreads.items():
        noise = np.random.default_rng([zlib.crc32(name.encode()), seed]).standard_normal(out[name].shape)
        drawn = base * np.exp(spread * noise) if base else spread * noise
        out[name] = jnp.asarray(drawn.astype(out[name].dtype))
    for name, factor in factors.items():
        out[name] = (out[name] * factor).astype(out[name].dtype)
    return out
```

```python
import concourse.bass as bass
from concourse import mybir
from contextlib import ExitStack

F32 = mybir.dt.float32
F16 = mybir.dt.float16
U32 = mybir.dt.uint32
I32 = mybir.dt.int32
ALU = mybir.AluOpType
ACT = mybir.ActivationFunctionType
AX = mybir.AxisListType

B, S, D = 8, 512, 256
H, DH = 16, 16
E, NSH, NEX = 128, 2, 18
NR, TOPK = NEX - NSH, 4
P = 128
TT = S // P
DC = D // P
G, GH = 4, 4
U = GH * TT
VW = DH + 1
HALF = NEX // 2
EPS = 1e-5
SCALE = DH ** -0.5
MINGATE = 0.25

LAG = {"max": 0, "maxT": 0, "exp": 0, "pv": 0, "h1T": 1, "qk": 1, "v": 1, "oT": -1, "onT": -1,
       "wo": -1, "h2T": -1, "logit": -1, "gateT": -1, "up": -1, "down": -1}
EXTRAS = {(0, 0): [("oT", 0), ("oT", 1)], (0, 1): [("oT", 2), ("oT", 3)],
          (0, 4): [("onT", 0), ("onT", 1)], (0, 6): [("h1T", 0), ("h1T", 1)],
          (0, 7): [("wo", 0), ("wo", 1)], (0, 9): [("qk", 0)], (0, 10): [("qk", 1)],
          (0, 11): [("qk", 2)], (0, 12): [("qk", 3), ("h2T", 0), ("h2T", 1)],
          (0, 13): [("v", 0), ("v", 1)], (0, 15): [("logit", 0)], (1, 4): [("gateT", 0)]}


def slot_order(s):
    out = []
    for u in range(U):
        out += EXTRAS.get((s, u), [])
        out.append(("max", (s + 1) * U + u) if s < 3 else ("max0", u))
        out.append(("exp", s * U + u))
        if s >= 2:
            n = HALF * (s - 2)
            out += [("down", n + c) for c in range(HALF) if (c * 14) // HALF + 2 == u]
    out.append(("maxT", s + 1) if s < 3 else ("maxT0", 0))
    if s in (1, 2):
        for c in range(HALF):
            out.append(("up", HALF * (s - 1) + c))
            if c % 2 == 1:
                out.append(("pv", s * TT + c // 2))
    else:
        out += [("pv", s * TT + kc) for kc in range(TT)]
    return out


ORDER = [(s, item) for s in range(G) for item in slot_order(s)]
V_KINDS = ("max", "max0", "maxT", "maxT0", "oT", "onT", "wo", "v", "logit", "gateT")
R_KINDS = ("exp", "h1T", "qk", "h2T", "up")
NV, NRB = 2, 3
PER = {"max": 64, "maxT": 4, "exp": 64, "oT": 4, "onT": 2, "wo": 2, "v": 2, "logit": 1, "gateT": 1,
       "h1T": 2, "qk": 4, "h2T": 2, "up": NEX, "pv": 4, "down": NEX}


def true_item(item):
    kind, n = item
    return {"max0": ("max", n, 1), "maxT0": ("maxT", 0, 1)}.get(kind, (kind, n, LAG.get(kind, 0)))


def ring(kinds, banks):
    seq = [item for _, item in ORDER if item[0] in kinds]
    assert len(seq) % banks == 0, len(seq)
    found = {}
    for j, item in enumerate(seq):
        users = [(seq[(j - banks * r) % len(seq)], (j - banks * r) // len(seq)) for r in range(1, 60)]
        found[item] = (j % banks, users)
    return found


RINGS = {**ring(V_KINDS, NV), **ring(R_KINDS, NRB)}


def exists(b):
    return not isinstance(b, int) or 0 <= b < B


def ffn_steps(c):
    return 3 * c - min(c, NSH)


def is_at(i, n):
    return isinstance(i, int) and i == n


def wait(eng, sem, per, b, k):
    value = b * per + k
    if isinstance(value, int) and value <= 0:
        return
    eng.wait_ge(sem, value)


def block_kernel(nc, x, c_t, wmod, wqkvo, bqk_in, bv, bo, w_up, w_down, router, out):
    q_d = nc.dram_tensor("q_parts", (2, DC, P, S), F16, kind="Internal").ap()
    k_d = nc.dram_tensor("k_parts", (2, DC, P, S), F16, kind="Internal").ap()
    gmod_d = nc.dram_tensor("gate_mods", (B, 2 * D), F32, kind="Internal").ap()
    tmod_d = nc.dram_tensor("feature_mods", (B, P, 8), F32, kind="Internal").ap()
    gate_d = nc.dram_tensor("gates_by_expert", (NR, S), F32, kind="Internal").ap()

    ctx = ExitStack()
    with ctx:
        def sb(name, shape, dt=F32):
            return ctx.enter_context(nc.sbuf_tensor(name, shape, dt))

        def sem(name):
            return ctx.enter_context(nc.semaphore(name))

        ident = sb("ident", [P, P])
        ident16 = sb("ident16", [P, P], F16)
        expert_no = sb("expert_no", [P, NR], I32)
        minus_half = sb("minus_half", [P, TT])
        w4 = [sb(f"wqkvo_{n}", [P, 4, DC, D], F16) for n in ("hi", "lo")]
        wr = [sb(f"router_{n}", [P, DC, NR], F16) for n in ("hi", "lo")]
        wu = [sb(f"up_{n}", [P, DC, NEX * E], F16) for n in ("hi", "lo")]
        wd = [sb(f"down_{n}", [P, NEX, D], F16) for n in ("hi", "lo")]
        bqk = sb("bqk", [P, 4])
        bv_all = sb("bv_all", [P, D])
        bo_all = sb("bo_all", [P, D])
        mod_pre = sb("mod_pre", [P, 8])
        mod_post = sb("mod_post", [P, 8])
        gmod = sb("gmod", [P, 2, D])
        x_pre = sb("x_pre", [P, TT, D])
        x_post = sb("x_post", [P, TT, D])
        rows = sb("rows", [P, TT, D])
        f_ring = sb("f_ring", [P, 2, S])
        h1 = [sb(f"h1_{n}", [P, DC, S], F16) for n in ("hi", "lo")]
        qk = [sb(f"qk_{n}", [P, 2, S], F16) for n in ("hi", "lo")]
        z = [sb(f"z_{n}", [P, DC, S], F16) for n in ("hi", "lo")]
        q_aug = [sb(f"q_aug{n}", [P, H // 2, S], F16) for n in range(2)]
        k_aug = [sb(f"k_aug{n}", [P, H // 2, S], F16) for n in range(2)]
        v_aug = [sb(f"v_aug{n}", [P, TT, H * VW + P // 4 - VW]) for n in range(2)]
        neg_max = sb("neg_max", [P, 2, TT, P], F16)
        probs = sb("probs", [P, U, S])
        o_raw = sb("o_raw", [P, G, S])
        act = [sb(f"act_{n}", [P, HALF, S], F16) for n in ("hi", "lo")]
        gelu = sb("gelu", [P, 4, S])
        gates = sb("gates", [P, 8, S])
        gate_rows = sb("gate_rows", [NR, S])
        stats = sb("stats", [P, TT, 6])
        mv = [sb(f"mean_var{n}", [P, TT, 2]) for n in range(2)]
        rstd = [sb(f"rstd{n}", [P, TT]) for n in range(2)]
        rsum = sb("rsum", [P, TT, H])
        logits = sb("logits", [P, TT, NR])
        top8 = sb("top8", [P, TT, 8])
        idx8 = sb("idx8", [P, TT, 8], U32)
        hit = sb("hit", [P, TT, TOPK, NR])
        chosen = sb("chosen", [P, TT, NR])
        shifted = sb("shifted", [P, TT, NR])
        e16 = sb("e16", [P, TT, NR])
        esum = sb("esum", [P, TT])
        zero_row = sb("zero_row", [1, S // 2], F16)
        ga_bo = gelu[:, 0, 0:D]

        wmod_st = probs[:, 0:6, :].rearrange("p a n -> p (a n)").rearrange("p (c n) -> p c n", c=DC)
        w4_st = o_raw[:, :, :].rearrange("p (w c) (a n) -> p (w c a) n", w=4, n=D)
        st_flat = gates[:, :, :].rearrange("p a n -> p (a n)")
        silu = probs[:, 6, 0:DC * B].rearrange("p (c b) -> p c b", c=DC)
        silu_t = probs[:, 7, 0:DC * B].rearrange("p (c b) -> p c b", c=DC)
        ct_st = probs[:, 8, 0:DC * B].rearrange("p (c b) -> p c b", c=DC)
        wr_st = probs[:, 9, 0:DC * NR].rearrange("p (c n) -> p c n", c=DC)
        tmod_st = probs[:, 10, 0:8 * B].rearrange("p (b k) -> p b k", b=B)
        gm = [probs[0:B, 11 + n, 0:2 * D] for n in range(3)]

        VB = [ctx.enter_context(nc.psum_tensor(f"vector_bank{n}", [P, S], F32)) for n in range(NV)]
        RB = [ctx.enter_context(nc.psum_tensor(f"scalar_bank{n}", [P, S], F32)) for n in range(NRB)]
        OB = ctx.enter_context(nc.psum_tensor("pv_bank", [P, S], F32))
        DB = [ctx.enter_context(nc.psum_tensor(f"down_bank{n}", [P, S], F32)) for n in range(2)]

        made = {k: sem(f"made_{k}") for k in PER}
        taken = {k: sem(f"taken_{k}") for k in PER}
        s_const = sem("constants_ready")
        s_passed = sem("waits_passed")
        s_w4, s_mod_in, s_small = sem("w4_loaded"), sem("mod_loaded"), sem("biases_loaded")
        s_w4s, s_silu, s_setup_mm, s_setup_v = sem("w4_split"), sem("silu_steps"), sem("mods_made"), sem("setup_vector")
        s_gm_st = sem("mods_stored")
        s_wst, s_wsp = sem("expert_weights_staged"), sem("expert_weights_split")
        s_xpre, s_mpre = sem("x_pre_loaded"), sem("mod_pre_loaded")
        s_xpost, s_mpost = sem("x_post_loaded"), sem("mods_post_loaded")
        s_ln1, s_ln2 = sem("ln1_steps"), sem("ln2_steps")
        s_rs1, s_rs2 = sem("rstd1_steps"), sem("rstd2_steps")
        s_h1lo, s_qklo, s_h2lo = sem("h1_lo"), sem("qk_lo"), sem("h2_lo")
        s_hi = sem("hi_parts_written")
        s_qkst, s_aug = [sem("qk0_stored"), sem("qk1_stored")], sem("score_operands_loaded")
        s_xg = sem("residual_plus_gated_bias")
        s_on = sem("normalised_steps")
        s_zsplit = sem("z_split_steps")
        s_res = sem("residual_steps")
        s_top, s_e16 = sem("router_steps"), sem("router_exp")
        s_gst, s_gld = sem("gates_stored"), sem("gates_loaded")
        s_gelu, s_ffn = sem("gelu_unused"), sem("expert_parts_made")
        s_fin, s_out = sem("final_steps"), sem("out_stored")
        s_aug0 = sem("score_operand_constants")

        def wait_apart(eng, sem, per, b, k):
            wait(eng, sem, per, b, k)
            if not isinstance(b, int):
                eng.sem_inc(s_passed, 1)

        block = ctx.enter_context(nc.Block())

        def bank(item):
            kind = item[0]
            n = RINGS[item][0]
            return (VB if kind in V_KINDS else RB)[n]

        def wait_bank(eng, item, i):
            for prev, back in RINGS[item][1]:
                kind, n, lag = true_item(prev)
                b = i + back + lag
                if exists(b) or (not isinstance(i, int)):
                    wait(eng, taken[kind], PER[kind], b, n + 1)
                    return

        def iterations(eng, body):
            body(-1, 1)
            body(0, 0)
            body(1, 1)
            with eng.Fori(0, 2) as j:
                body(j * 2 + 2, 0)
                body(j * 2 + 3, 1)
            body(6, 0)
            body(7, 1)
            body(8, 0)

        def items(i, s):
            for item in slot_order(s):
                kind, n, lag = true_item(item)
                if exists(i + lag):
                    yield item, kind, n, i + lag


        @block.sync
        def _(sp):
            for w in range(4):
                sp.dma_start(w4_st[:, 2 * w:2 * w + 2, :], wqkvo[w].rearrange("(c p) n -> p c n", c=DC)).then_inc(s_w4, 16)
            sp.dma_start(ct_st, c_t.rearrange("(c p) b -> p c b", c=DC)).then_inc(s_mod_in, 16)
            sp.dma_start(wmod_st, wmod.rearrange("(c p) n -> p c n", c=DC)).then_inc(s_mod_in, 16)
            sp.dma_start(wr_st, router.rearrange("(c p) n -> p c n", c=DC)).then_inc(s_mod_in, 16)
            sp.dma_start(bqk[:], bqk_in).then_inc(s_small, 16)
            sp.dma_start(bv_all[:], bv.partition_broadcast(P)).then_inc(s_small, 16)
            sp.dma_start(bo_all[:], bo.partition_broadcast(P)).then_inc(s_small, 16)
            sp.wait_ge(s_setup_v, 10)
            sp.dma_start(tmod_d.rearrange("b p k -> p b k"), tmod_st).then_inc(s_gm_st, 16)
            sp.dma_start(gmod_d, gm[2]).then_inc(s_gm_st, 16)
            sp.wait_ge(s_gm_st, 32)

            def body(i, par):
                b = i + 1
                if exists(b):
                    wait_apart(sp, s_ln1, 12, b, 0)
                    sp.dma_start(x_pre[:], x[b].rearrange("(t p) d -> p t d", t=TT)).then_inc(s_xpre, 16)
                    wait_apart(sp, taken["h1T"], 2, b, 0)
                    sp.dma_start(mod_pre[:], tmod_d[b]).then_inc(s_mpre, 16)
                b = i - 1
                if exists(b):
                    wait_apart(sp, s_out, 16, b, 0)
                    sp.dma_start(x_post[:], x[b].rearrange("(t p) d -> p t d", t=TT)).then_inc(s_xpost, 16)
                    wait_apart(sp, taken["h2T"], 2, b, 0)
                    sp.dma_start(mod_post[:], tmod_d[b]).then_inc(s_mpost, 16)
                    wait_apart(sp, s_fin, 4, b, 0)
                    sp.dma_start(gmod[:, :, :], gmod_d[b].rearrange("(a n) -> a n", a=2).partition_broadcast(P)).then_inc(s_mpost, 16)
                b = i + 1
                if exists(b):
                    qa, ka = q_aug[1 - par], k_aug[1 - par]
                    for n in range(4):
                        dst = (q_d, k_d)[n // 2]
                        wait_apart(sp, s_qklo, 4, b, n + 1)
                        if n == 0:
                            wait_apart(sp, s_aug, 16 * 14, b, 0)
                        for part in range(2):
                            sp.dma_start(dst[part, n % 2], qk[part][:, n % 2, :]).then_inc(s_qkst[n % 2], 16)
                        if n % 2 == 1:
                            for m in range(2):
                                wait_apart(sp, s_qkst[m], 64, b, 32 * (n // 2 + 1))
                            if n == 1:
                                wait_apart(sp, made["exp"], 64, i, 0)
                                wait_apart(sp, made["max"], 64, i, 0)
                            aug = (qa, ka)[n // 2]
                            for par2 in range(2):
                                for row, part in ((0, 0), (16, n // 2 == 0), (48, n // 2)):
                                    src = dst[int(part)].rearrange("c (p two d) t -> two d (c p) t", two=2, d=DH)[par2]
                                    at = 64 * par2 + row
                                    sp.dma_start(aug[at:at + DH, :, :], src).then_inc(s_aug, 16)
                    for par2 in range(2):
                        sp.dma_start(qa[64 * par2 + 32:64 * par2 + 33, :, :].rearrange("r a (b n) -> r (a b) n", b=2),
                                     zero_row[0:1, :].unsqueeze(1).broadcast_to([1, H, S // 2])).then_inc(s_aug, 16)
                b = i - 1
                if is_at(i, 0):
                    for n in range(4):
                        if n:
                            sp.wait_ge(s_wsp, 2 * n)
                        src = w_up[P * n:P * n + P, :] if n < 2 else w_down[HALF * (n - 2):HALF * (n - 1)].rearrange("e p d -> p e d")
                        dst = st_flat[:, 0:HALF * D] if n < 2 else st_flat[:, 0:HALF * D].rearrange("p (e d) -> p e d", e=HALF)
                        sp.dma_start(dst, src).then_inc(s_wst, 16)
                if exists(b):
                    wait_apart(sp, taken["gateT"], 1, b, 1)
                    wait_apart(sp, s_gld, 32, b, 0)
                    sp.dma_start(gate_d, gate_rows[:, :]).then_inc(s_gst, 16)
                    wait_apart(sp, s_gst, 16, b, 16)
                    for n in range(2):
                        if n == 0:
                            wait_apart(sp, s_ffn, ffn_steps(NEX), b, 0)
                        else:
                            wait_apart(sp, s_ffn, ffn_steps(NEX), b, ffn_steps(NSH + 8))
                        sp.dma_start(gates[:, :, :], gate_d[8 * n:8 * n + 8, :].partition_broadcast(P)).then_inc(s_gld, 16)
                    wait_apart(sp, s_fin, 4, b, 4)
                    sp.dma_start(out[b].rearrange("(t p) d -> p t d", t=TT), x_post[:]).then_inc(s_out, 16)

            iterations(sp, body)
            sp.wait_ge(s_out, 16 * B)
            sp.wait_ge(s_gst, 16 * B)
            for m in range(2):
                sp.wait_ge(s_qkst[m], 64 * B)

        @block.gpsimd
        def _(pool):
            pool.memset(ident[:], 0.0).then_inc(s_const, 1)
            pool.memset(ident16[:], 0.0).then_inc(s_const, 1)
            pool.memset(minus_half[:], -0.5).then_inc(s_const, 1)
            pool.iota(expert_no[:], [[1, NR]], base=0, channel_multiplier=0).then_inc(s_const, 1)
            pool.wait_ge(s_const, 4)
            for m in (ident, ident16):
                pool.affine_select(out=m[:], in_=m[:], compare_op=ALU.not_equal, fill=1.0, base=0,
                                   pattern=[[-1, P]], channel_multiplier=1).then_inc(s_const, 1)
            pool.memset(neg_max[:], 0.0).then_inc(s_const, 1)
            pool.memset(zero_row[:], 0.0).then_inc(s_const, 1)

            def power(b, m, r, s_stats, s_rs, first):
                wait_apart(pool, s_stats, 12, b, 8)
                pool.tensor_scalar(r[:], m[:, :, 1], EPS, None, ALU.add).then_inc(s_rs, 1)
                wait(pool, s_rs, 2, b, 1)
                pool.tensor_tensor(r[:], r[:], minus_half[:], ALU.pow).then_inc(s_rs, 1)

            def lo_part(kind, n, b, fslot, hi, lo, s_lo, per):
                wait(pool, taken[kind], PER[kind], b, n + 1)
                pool.tensor_tensor(lo, f_ring[:, fslot, :], hi, ALU.subtract).then_inc(s_lo, 1)

            def body(i, par):
                if exists(i + 1):
                    power(i + 1, mv[0], rstd[0], s_ln1, s_rs1, i == -1)
                b = i - 1
                if exists(b):
                    wait(pool, s_mpost, 32, b, 32)
                    wait(pool, s_ffn, ffn_steps(NEX), b, 0)
                    pool.tensor_tensor(ga_bo, gmod[:, 0, :], bo_all[:], ALU.mult).then_inc(s_xg, 1)
                    wait(pool, s_xg, 2, b, 1)
                    wait(pool, s_xpost, 16, b, 16)
                    pool.tensor_tensor(x_post[:], x_post[:], ga_bo.unsqueeze(1).broadcast_to([P, TT, D]), ALU.add).then_inc(s_xg, 1)
                if exists(i + 1):
                    for n in range(2):
                        if n == 0:
                            wait(pool, made["v"], 2, i + 1, 0)
                        lo_part("h1T", n, i + 1, n, h1[0][:, n, :], h1[1][:, n, :], s_h1lo, 2)
                if exists(b):
                    power(b, mv[1], rstd[1], s_ln2, s_rs2, False)
                if exists(i + 1):
                    for n in range(4):
                        lo_part("qk", n, i + 1, n % 2, qk[0][:, n % 2, :], qk[1][:, n % 2, :], s_qklo, 4)
                if exists(b):
                    for n in range(2):
                        lo_part("h2T", n, b, n, z[0][:, n, :], z[1][:, n, :], s_h2lo, 2)
                if is_at(i, 0):
                    for n in range(4):
                        hi, lo = (w[:, n, :] if n < 2 else w[:, HALF * (n - 2):HALF * (n - 1), :].rearrange("p e d -> p (e d)")
                                  for w in ((wu if n < 2 else wd)))
                        src = st_flat[:, 0:HALF * D]
                        pool.wait_ge(s_wst, 16 * (n + 1))
                        pool.tensor_copy(hi, src).then_inc(s_wsp, 1)
                        pool.wait_ge(s_wsp, 2 * n + 1)
                        pool.tensor_tensor(lo, src, hi, ALU.subtract).then_inc(s_wsp, 1)
                if exists(b):
                    for c in range(NEX):
                        g = gelu[:, c % 4, :]
                        hi, lo = (a[:, c % HALF, :] for a in act)
                        wait(pool, taken["up"], NEX, b, c + 1)
                        if c >= NSH:
                            if c == NSH or c == NSH + 8:
                                wait(pool, s_gld, 32, b, 16 if c == NSH else 32)
                            pool.tensor_tensor(g, g, gates[:, (c - NSH) % 8, :], ALU.mult).then_inc(s_ffn, 1)
                            wait(pool, s_ffn, ffn_steps(NEX), b, ffn_steps(c) + 1)
                        if c % HALF == 0:
                            wait(pool, made["down"], NEX, b, c)
                        if not isinstance(b, int):
                            pool.sem_inc(s_passed, 1)
                        pool.tensor_copy(hi, g).then_inc(s_ffn, 1)
                        wait(pool, s_ffn, ffn_steps(NEX), b, ffn_steps(c + 1) - 1)
                        pool.tensor_tensor(lo, g, hi, ALU.subtract).then_inc(s_ffn, 1)

            iterations(pool, body)

        @block.scalar
        def _(scalar):
            scalar.wait_ge(s_mod_in, 16 * 3)
            scalar.activation(silu_t, ct_st, ACT.Exp, scale=-1.0).then_inc(s_silu, 1)
            scalar.wait_ge(s_small, 48)

            def split_out(kind, n, b, src, hi, f, scale, bias):
                scalar.activation(hi, src, ACT.Identity, bias=bias, scale=scale)
                scalar.activation(f, src, ACT.Identity, bias=bias, scale=scale).then_inc(taken[kind], 1)

            def body(i, par):
                for s in range(G):
                    for item, kind, n, b in items(i, s):
                        if item[0] not in R_KINDS:
                            continue
                        src = bank(item)
                        wait(scalar, made[kind], PER[kind], b, n + 1)
                        if kind == "exp":
                            if n % U == 0:
                                wait(scalar, made["pv"], 4, b, n // U)
                            scalar.activation(probs[:, n % U, :], src[:], ACT.Exp, scale=SCALE).then_inc(taken[kind], 1)
                        elif kind == "h1T":
                            if n == 0:
                                wait(scalar, s_mpre, 16, b, 16)
                                wait(scalar, made["v"], 2, b, 0)
                            wait(scalar, s_qklo, 4, b, 0)
                            split_out(kind, n, b, src[:], h1[0][:, n, :], f_ring[:, n, :],
                                      mod_pre[:, 2 + n:3 + n], mod_pre[:, n:n + 1])
                        elif kind == "qk":
                            if n < 2:
                                wait(scalar, s_h1lo, 2, b, 2)
                                wait(scalar, s_qkst[n], 64, b, 0)
                            else:
                                wait(scalar, s_qklo, 4, b, n - 1)
                                wait(scalar, s_qkst[n - 2], 64, b, 32)
                            scalar.activation(qk[0][:, n % 2, :], src[:], ACT.Identity, bias=bqk[:, n:n + 1])
                            scalar.activation(f_ring[:, n % 2, :], src[:], ACT.Identity, bias=bqk[:, n:n + 1]).then_inc(taken[kind], 1)
                        elif kind == "h2T":
                            if n == 0:
                                wait(scalar, s_mpost, 32, b, 32)
                            if exists(i + 1):
                                wait(scalar, s_qklo, 4, i + 1, 4)
                            wait(scalar, made["wo"], 2, b, 2)
                            split_out(kind, n, b, src[:], z[0][:, n, :], f_ring[:, n, :],
                                      mod_post[:, 6 + n:7 + n], mod_post[:, 4 + n:5 + n])
                        elif kind == "up":
                            wait(scalar, s_ffn, ffn_steps(NEX), b, ffn_steps(max(n - 3, 0)))
                            scalar.activation(gelu[:, n % 4, :], src[:], ACT.Gelu).then_inc(taken[kind], 1)
                    if s == 0 and exists(i - 1):
                        wait(scalar, s_top, 15, i - 1, 9)
                        scalar.activation(e16[:], shifted[:], ACT.Exp).then_inc(s_e16, 1)

            iterations(scalar, body)

        @block.vector
        def _(dve):
            w4f = w4_st.rearrange("p a n -> p (a n)")
            hi4, lo4 = (w[:].rearrange("p w c n -> p (w c n)") for w in w4)
            dve.wait_ge(s_w4, 64)
            dve.tensor_copy(hi4, w4f).then_inc(s_w4s, 1)
            for n in range(2):
                dve.memset(q_aug[n][:].bitcast(U32), 0).then_inc(s_aug0, 1)
                dve.memset(k_aug[n][:].bitcast(U32), 0).then_inc(s_aug0, 1)
                dve.memset(v_aug[n][:], 1.0).then_inc(s_aug0, 1)
            dve.wait_ge(s_w4s, 1)
            dve.tensor_tensor(lo4, w4f, hi4, ALU.subtract).then_inc(s_w4s, 1)
            dve.wait_ge(s_aug0, 6)
            for n in range(2):
                for p in (32, 96):
                    dve.memset(k_aug[n][p:p + 1, :, :], 1.0).then_inc(s_aug0, 1)
            dve.wait_ge(s_mod_in, 48)
            dve.tensor_copy(wr[0][:], wr_st).then_inc(s_setup_v, 1)
            dve.wait_ge(s_setup_v, 1)
            dve.tensor_tensor(wr[1][:], wr_st, wr[0][:], ALU.subtract).then_inc(s_setup_v, 1)
            dve.wait_ge(s_silu, 1)
            dve.tensor_scalar(silu_t, silu_t, 1.0, None, ALU.add).then_inc(s_silu, 1)
            dve.wait_ge(s_silu, 2)
            dve.reciprocal(silu_t, silu_t).then_inc(s_silu, 1)
            dve.wait_ge(s_silu, 3)
            dve.tensor_tensor(silu, silu_t, ct_st, ALU.mult).then_inc(s_silu, 1)
            dve.wait_ge(s_setup_mm, 1)
            src = DB[0][:, 0:8 * B].rearrange("p (k b) -> p b k", k=8)
            for n, add in ((0, 0.0), (2, 1.0), (4, 0.0), (6, 1.0)):
                dve.tensor_scalar(tmod_st[:, :, n:n + 2], src[:, :, n:n + 2], add, None, ALU.add).then_inc(s_setup_v, 1)
            g = DB[1][0:B, 0:2 * D]
            dve.tensor_scalar(gm[0], g, 0.0, 2.0, ALU.is_ge, ALU.mult).then_inc(s_setup_v, 1)
            dve.tensor_scalar(gm[1], g, -1.0, MINGATE, ALU.mult, ALU.max).then_inc(s_setup_v, 1)
            dve.wait_ge(s_setup_v, 8)
            dve.tensor_tensor(gm[1], gm[1], g, ALU.max).then_inc(s_setup_v, 1)
            dve.wait_ge(s_setup_v, 9)
            dve.scalar_tensor_tensor(gm[2], gm[0], -1.0, gm[1], ALU.add, ALU.mult).then_inc(s_setup_v, 1)

            def ln_stats(src, m, s_ln, b, ready, per, k):
                for t in range(TT):
                    if t == 0:
                        wait(dve, ready, per, b, k)
                    dve.bn_stats(stats[:, t, :], src[:, t, :]).then_inc(s_ln, 1)
                for t in range(TT):
                    if t == 0:
                        wait_apart(dve, s_ln, 12, b, 4)
                    dve.bn_aggr(m[:, t, :], stats[:, t, :]).then_inc(s_ln, 1)

            def ln_rows(src, m, r, s_ln, s_rs, b):
                wait(dve, s_rs, 2, b, 2)
                for t in range(TT):
                    dve.tensor_scalar(rows[:, t, :], src[:, t, :], m[:, t, 0:1], r[:, t:t + 1],
                                      ALU.subtract, ALU.mult).then_inc(s_ln, 1)

            def top_four(b):
                w = lambda k: wait_apart(dve, s_top, 15, b, k)
                wait_apart(dve, taken["logit"], 1, b, 1)
                for t in range(TT):
                    dve.max(top8[:, t, :], logits[:, t, :]).then_inc(s_top, 1)
                w(4)
                for t in range(TT):
                    dve.max_index(idx8[:, t, :], top8[:, t, :], logits[:, t, :]).then_inc(s_top, 1)
                dve.tensor_tensor(shifted[:], logits[:], top8[:, :, 0:1].broadcast_to([P, TT, NR]),
                                  ALU.subtract).then_inc(s_top, 1)
                w(8)
                dve.tensor_tensor(hit[:], idx8[:, :, 0:TOPK].unsqueeze(3).broadcast_to([P, TT, TOPK, NR]),
                                  expert_no[:].unsqueeze(1).unsqueeze(1).broadcast_to([P, TT, TOPK, NR]),
                                  ALU.is_equal).then_inc(s_top, 1)
                w(10)
                dve.tensor_reduce(chosen[:], hit[:].rearrange("p t k e -> p t e k"), AX.X, ALU.add).then_inc(s_top, 1)

            def gate_values(b):
                w = lambda k: wait_apart(dve, s_top, 15, b, k)
                wait(dve, s_e16, 1, b, 1)
                dve.tensor_reduce(esum[:], e16[:], AX.X, ALU.add).then_inc(s_top, 1)
                w(12)
                dve.reciprocal(esum[:], esum[:]).then_inc(s_top, 1)
                w(11)
                dve.tensor_tensor(chosen[:], chosen[:], e16[:], ALU.mult).then_inc(s_top, 1)
                w(14)
                dve.tensor_tensor(chosen[:], chosen[:], esum[:].unsqueeze(2).broadcast_to([P, TT, NR]),
                                  ALU.mult).then_inc(s_top, 1)

            def body(i, par):
                nb, pb = i + 1, i - 1
                for s in range(G):
                    for item, kind, n, b in items(i, s):
                        if item == ("oT", 2) or (item == ("h1T", 0) and not exists(pb)):
                            if exists(nb):
                                ln_stats(x_pre, mv[0], s_ln1, nb, s_xpre, 16, 16)
                        if item == ("h1T", 0):
                            if exists(pb):
                                wait(dve, made["onT"], 2, pb, 2)
                            ln_rows(x_pre, mv[0], rstd[0], s_ln1, s_rs1, nb)
                        if item == ("h2T", 0):
                            if exists(nb):
                                wait(dve, made["h1T"], 2, nb, 2)
                            ln_rows(x_post, mv[1], rstd[1], s_ln2, s_rs2, pb)
                        if item[0] not in V_KINDS:
                            continue
                        src = bank(item)
                        wait(dve, made[kind], PER[kind], b, n + 1)
                        done = taken[kind]
                        if kind == "max":
                            u = n % U
                            dve.tensor_reduce(neg_max[:, u // 8, (u // 2) % TT, 32 + 64 * (u % 2):33 + 64 * (u % 2)],
                                              src[:], AX.X, ALU.max, negate=True).then_inc(done, 1)
                        elif kind == "maxT":
                            qa = q_aug[par if b is i or n else 1 - par]
                            if item[0] == "maxT0":
                                qa = q_aug[1 - par]
                            srcT = src[:].bitcast(F16).rearrange("p (a n) -> p a n", a=2)
                            dve.tensor_copy(qa[32:33, 2 * n:2 * n + 2, :], srcT[32:33, :, :])
                            dve.tensor_copy(qa[96:97, 2 * n:2 * n + 2, :], srcT[96:97, :, :]).then_inc(done, 1)
                        elif kind == "oT":
                            o = src[:].rearrange("p (h w) -> p h w", h=H)
                            if n == 0 and exists(b - 1):
                                wait(dve, made["h2T"], 2, b, 0)
                            dve.reciprocal(rsum[:, n, :], o[:, :, 0]).then_inc(s_on, 1)
                            wait(dve, s_on, 4, b, n + 1)
                            dve.tensor_tensor(rows[:, n, :].rearrange("p (h w) -> p h w", h=H), o[:, :, 1:VW],
                                              rsum[:, n, :].unsqueeze(2).broadcast_to([P, H, DH]), ALU.mult).then_inc(done, 1)
                        elif kind == "onT":
                            if n == 0:
                                wait(dve, made["up"], NEX, b, 0)
                                wait(dve, made["logit"], 1, b, 0)
                            dve.tensor_copy(z[0][:, n, :], src[:]).then_inc(s_zsplit, 1)
                            wait(dve, s_zsplit, 2, b, n + 1)
                            dve.tensor_tensor(z[1][:, n, :], src[:], z[0][:, n, :], ALU.subtract).then_inc(done, 1)
                        elif kind == "wo":
                            if n == 0:
                                wait(dve, s_xg, 2, b, 2)
                            pv2 = src[:].rearrange("p (t d) -> p t d", t=2)
                            sc = gelu[:, 2 + n, :].rearrange("p (t d) -> p t d", t=2)
                            dve.tensor_tensor(sc, pv2, gmod[:, 0:1, :].broadcast_to([P, 2, D]), ALU.mult).then_inc(s_res, 1)
                            wait(dve, s_res, 2, b, n + 1)
                            dve.tensor_tensor(x_post[:, 2 * n:2 * n + 2, :], x_post[:, 2 * n:2 * n + 2, :], sc,
                                              ALU.add).then_inc(done, 1)
                            if n == 1:
                                ln_stats(x_post, mv[1], s_ln2, b, taken["wo"], 2, 2)
                        elif kind == "v":
                            va = v_aug[1 - par]
                            if n == 0:
                                dve.wait_ge(s_aug0, 10)
                                wait(dve, made["pv"], 4, i, 0)
                            for t in range(2):
                                ins = dve.tensor_tensor(
                                    va[:, 2 * n + t, 0:H * VW].rearrange("p (h w) -> p h w", h=H)[:, :, 1:VW],
                                    src[:, t * D:(t + 1) * D].rearrange("p (h w) -> p h w", h=H),
                                    bv_all[:].rearrange("p (h w) -> p h w", h=H), ALU.add)
                            ins.then_inc(done, 1)
                        elif kind == "logit":
                            dve.tensor_copy(logits[:].rearrange("p t e -> p (t e)"), src[:, 0:TT * NR]).then_inc(done, 1)
                            top_four(b)
                        elif kind == "gateT":
                            wait(dve, s_gst, 16, b, 0)
                            dve.tensor_copy(gate_rows[:, :], src[0:NR, :]).then_inc(done, 1)
                    if s == 0 and exists(pb):
                        gate_values(pb)
                    b = i
                    if exists(b):
                        wait(dve, made["pv"], 4, b, s + 1)
                        wait(dve, made["oT"], 4, b, 0)
                        dve.tensor_copy(o_raw[:, s, :], OB[:]).then_inc(taken["pv"], 1)
                if exists(pb):
                    wait(dve, made["down"], NEX, pb, NEX)
                    for n in range(2):
                        sc = rows[:, 2 * n:2 * n + 2, :]
                        dve.tensor_tensor(sc, DB[n][:].rearrange("p (t d) -> p t d", t=2),
                                          gmod[:, 1:2, :].broadcast_to([P, 2, D]), ALU.mult).then_inc(s_fin, 1)
                    for n in range(2):
                        wait(dve, s_fin, 4, pb, n + 1)
                        xs = x_post[:, 2 * n:2 * n + 2, :]
                        dve.tensor_tensor(xs, xs, rows[:, 2 * n:2 * n + 2, :], ALU.add).then_inc(s_fin, 1)

            iterations(dve, body)

        @block.tensor
        def _(pe):
            def split_product(dst, pairs, last_sem=None):
                terms = [(a, b) for st, mo in pairs for a, b in ((st[0], mo[0]), (st[0], mo[1]), (st[1], mo[0]))]
                for n, (a, b) in enumerate(terms):
                    ins = pe.matmul(dst, a, b, start=n == 0, stop=n == len(terms) - 1)
                return ins

            pe.wait_ge(s_silu, 4)
            for k, col in enumerate((0, D, 3 * D, 4 * D)):
                for half in range(2):
                    for c in range(DC):
                        o = DB[0][:, (2 * k + half) * B:(2 * k + half + 1) * B]
                        pe.matmul(o, wmod_st[:, c, col + P * half:col + P * half + P], silu[:, c, :],
                                  start=c == 0, stop=c == DC - 1)
            for k, col in enumerate((2 * D, 5 * D)):
                for c in range(DC):
                    ins = pe.matmul(DB[1][0:B, D * k:D * k + D], silu[:, c, :], wmod_st[:, c, col:col + D],
                                    start=c == 0, stop=c == DC - 1)
            ins.then_inc(s_setup_mm, 1)
            pe.wait_ge(s_const, 8)
            pe.wait_ge(s_w4s, 2)

            def unit(n):
                u = n % U
                return (n // U) * 2 + u // 8, 64 * (u % 2), (u // 2) % TT

            def body(i, par):
                for s in range(G):
                    for item, kind, n, b in items(i, s):
                        if kind in V_KINDS or kind in R_KINDS:
                            wait_bank(pe, item, i)
                            dst = bank(item)
                        sig = made[kind]
                        if kind in ("max", "exp"):
                            ahead = item[0] == "max0"
                            qa, ka = q_aug[1 - par if ahead else par], k_aug[1 - par if ahead else par]
                            pair, at, t = unit(n)
                            if item == ("max0", 0):
                                wait(pe, s_aug, 16 * 14, b, 16 * 14)
                            if kind == "exp" and n % U == 0:
                                wait(pe, taken["maxT"], 4, b, n // U + 1)
                            st, mo = (qa, ka) if kind == "max" else (ka, qa)
                            pe.matmul(dst[:], st[at:at + 64, pair, t * P:(t + 1) * P], mo[at:at + 64, pair, :],
                                      start=True, stop=True).then_inc(sig, 1)
                        elif kind == "maxT":
                            wait(pe, taken["max"], PER["max"], b, U * (n + 1))
                            d16 = dst[:].bitcast(F16)
                            for a in range(2):
                                for t in range(TT):
                                    o = (a * TT + t) * P
                                    ins = pe.transpose(d16[:, o:o + P], neg_max[:, a, t, :], ident16[:])
                            ins.then_inc(sig, 1)
                        elif kind == "pv":
                            g, kc = divmod(n, TT)
                            if kc == 0:
                                if g == 0:
                                    wait(pe, taken["v"], 2, b, 2)
                                wait(pe, taken["pv"], 4, b, g)
                            if kc == 0:
                                wait(pe, taken["exp"], 64, b, U * (g + 1))
                            for j in range(GH):
                                h = g * GH + j
                                u = (j // 2) * 8 + kc * 2 + j % 2
                                ins = pe.matmul(OB[32 * j:32 * j + 32, :], v_aug[par][:, kc, h * VW:h * VW + 32],
                                                probs[:, u, :], start=kc == 0, stop=kc == TT - 1)
                            if kc == TT - 1:
                                ins.then_inc(sig, 1)
                        elif kind == "h1T" or kind == "h2T" or kind == "onT":
                            if n == 0:
                                if kind == "h1T":
                                    wait(pe, s_ln1, 12, b, 12)
                                elif kind == "h2T":
                                    wait(pe, s_ln2, 12, b, 12)
                                else:
                                    wait(pe, taken["oT"], 4, b, 4)
                            for t in range(TT):
                                ins = pe.transpose(dst[:, t * P:(t + 1) * P], rows[:, t, n * P:(n + 1) * P], ident[:])
                            ins.then_inc(sig, 1)
                        elif kind == "oT":
                            if n == 0:
                                wait(pe, taken["pv"], 4, b, 4)
                            for g in range(G):
                                ins = pe.transpose(dst[:, g * P:(g + 1) * P], o_raw[:, g, n * P:(n + 1) * P], ident[:])
                            ins.then_inc(sig, 1)
                        elif kind == "qk":
                            if n == 0:
                                wait(pe, s_h1lo, 2, b, 2)
                            w, m = divmod(n, 2)
                            split_product(dst[:], [([p[:, w, c, m * P:(m + 1) * P] for p in w4],
                                                    [p[:, c, :] for p in h1]) for c in range(DC)]).then_inc(sig, 1)
                        elif kind == "v" or kind == "wo":
                            a = h1 if kind == "v" else z
                            if n == 0 and kind == "wo":
                                wait(pe, taken["onT"], 2, b, 2)
                            for t in range(2):
                                tok = (2 * n + t) * P
                                ins = split_product(dst[:, t * D:(t + 1) * D],
                                                    [([p[:, c, tok:tok + P] for p in a],
                                                      [p[:, 2 if kind == "v" else 3, c, :] for p in w4]) for c in range(DC)])
                            ins.then_inc(sig, 1)
                        elif kind == "logit":
                            wait(pe, s_h2lo, 2, b, 2)
                            for t in range(TT):
                                ins = split_product(dst[:, t * NR:(t + 1) * NR],
                                                    [([p[:, c, t * P:(t + 1) * P] for p in z],
                                                      [p[:, c, :] for p in wr]) for c in range(DC)])
                            ins.then_inc(sig, 1)
                        elif kind == "gateT":
                            wait(pe, s_top, 15, b, 15)
                            for t in range(TT):
                                ins = pe.transpose(dst[0:NR, t * P:(t + 1) * P], chosen[:, t, :], ident[:])
                            ins.then_inc(sig, 1)
                        elif kind == "up":
                            if n == 0:
                                pe.wait_ge(s_wsp, 8)
                            split_product(dst[:], [([p[:, c, n * E:(n + 1) * E] for p in wu],
                                                    [p[:, c, :] for p in z]) for c in range(DC)]).then_inc(sig, 1)
                        elif kind == "down":
                            if n == 0:
                                wait(pe, s_fin, 4, b, 0)
                            wait(pe, s_ffn, ffn_steps(NEX), b, ffn_steps(n + 1))
                            for t in range(TT):
                                o = DB[t // 2][:, (t % 2) * D:(t % 2 + 1) * D]
                                for k, (a, w) in enumerate(((0, 0), (0, 1), (1, 0))):
                                    ins = pe.matmul(o, act[a][:, n % HALF, t * P:(t + 1) * P], wd[w][:, n, :],
                                                    start=n == 0 and k == 0 and t % 2 == 0,
                                                    stop=n == NEX - 1 and k == 2, skip_group_check=True)
                            ins.then_inc(sig, 1)

            iterations(pe, body)


def kernel(**inputs):
    import numpy as np
    import concourse.bacc as bacc
    from concourse import mybir as mb
    from concourse.bass_utils import run_bass_kernel_spmd as run

    a = {k[3:]: np.asarray(v) for k, v in inputs.items()}
    laid = {
        "x": a["attn_x"], "c_t": a["c"].T, "wmod": a["wmod"],
        "wqkvo": np.stack([a["attn_wq"], a["attn_wk"], a["attn_wv"], a["attn_wo"]]),
        "bqk": np.stack([a["attn_bq"], a["attn_bk"]]).reshape(4, P).T, "bv": a["attn_bv"], "bo": a["attn_bo"],
        "w_up": np.concatenate([a["ffn_shared_up"], a["ffn_routed_up"]]).reshape(NEX * E, D).T,
        "w_down": np.concatenate([a["ffn_shared_down"], a["ffn_routed_down"]]).transpose(0, 2, 1),
        "router": a["ffn_router_w"].T,
    }
    nc = bacc.Bacc("TRN2", target_bir_lowering=False, num_devices=1)
    arrays, args = {}, []
    for name, v in laid.items():
        v = np.ascontiguousarray(v)
        arrays[f"in_{name}"] = v
        args.append(nc.dram_tensor(f"in_{name}", v.shape, mb.dt.from_np(v.dtype), kind="ExternalInput").ap())
    out = nc.dram_tensor("out_0", (B, S, D), mb.dt.float32, kind="ExternalOutput").ap()
    block_kernel(nc, *args, out)
    r = run(nc, [arrays], core_ids=[0])
    return r.results[0]["out_0"]
```

```python
import concourse.bass as bass
from concourse import mybir
from contextlib import ExitStack

F32 = mybir.dt.float32
F16 = mybir.dt.float16
U32 = mybir.dt.uint32
I32 = mybir.dt.int32
ALU = mybir.AluOpType
ACT = mybir.ActivationFunctionType
AX = mybir.AxisListType

B, S, D = 8, 512, 256
H, DH = 16, 16
E, NSH, NEX = 128, 2, 18
NR, TOPK = NEX - NSH, 4
P = 128
TT = S // P
DC = D // P
G, GH = 4, 4
U = GH * TT
VW = DH + 1
NW, WL = 8, 2 * DC * NEX * E // 8
NST = 3
EPS = 1e-5
SCALE = DH ** -0.5
MINGATE = 0.25

SETS = [0, 5, 10, 14, 18]
SETLEN = max(b - a for a, b in zip(SETS, SETS[1:]))
SET_OF = [sum(c >= e for e in SETS[1:]) for c in range(NEX)]
UP_SET = {2: 0, 3: 1, 0: 2, 1: 3}
DOWN_SET = {3: 0, 0: 1, 1: 2, 2: 3}
EXTRAS = {(0, 2): [("oT", 0)], (0, 3): [("oT", 1)], (0, 4): [("oT", 2)], (0, 5): [("oT", 3)],
          (0, 7): [("onT", 0)], (0, 8): [("onT", 1)], (0, 9): [("stats1", 0)], (0, 11): [("wo", 0)],
          (0, 13): [("wo", 1)], (0, 17): [("stats2", 0)], (0, 19): [("rows2", 0)],
          (1, 0): [("h2T", 0)], (1, 2): [("h2T", 1)], (1, 3): [("rows1", 0)], (1, 5): [("h1T", 0)],
          (1, 6): [("h1T", 1)], (1, 7): [("logit", 0)], (1, 8): [("top", 0)],
          (1, 10): [("qk", 0)], (1, 12): [("e16", 0)], (1, 13): [("qk", 1)], (1, 14): [("gates", 0)],
          (2, 2): [("gateT", 0)], (2, 4): [("qk", 2)], (2, 6): [("qk", 3)], (2, 18): [("final", 0)],
          (2, 8): [("v", 0)], (2, 9): [("v", 1)]}
WSPLIT = {(-1, 2, 10): 0, (-1, 2, 11): 1, (-1, 2, 12): 2, (0, 0, 3): 3, (0, 0, 7): 4, (0, 0, 11): 5,
          (0, 2, 11): 6, (0, 3, 9): 7}
for (_, _s, _u), _n in WSPLIT.items():
    EXTRAS[_s, _u] = EXTRAS.get((_s, _u), []) + [("wsplit", _n)]
NO_MAX = {0: (0, 1, 9, 15), 1: (0, 4, 8, 15), 2: (0, 3, 8, 15), 3: (0, 4, 7, 15)}


def slot_order(s):
    out = []
    maxima = [("max", (s + 1) * U + u) if s < 3 else ("max0", u) for u in range(U)]
    downs = [("down", d) for d in range(TT * SETS[DOWN_SET[s]], TT * SETS[DOWN_SET[s] + 1])]
    ups = [("up", c) for c in range(*SETS[UP_SET[s]:UP_SET[s] + 2])]
    for u in range(U):
        out += EXTRAS.get((s, u), [])
        if u not in NO_MAX[s]:
            out.append(maxima.pop(0))
        out.append(("exp", s * U + u))
        left = U - 1 - u
        while u and downs and len(downs) * (U - 1) > left * TT * SETLEN:
            out.append(downs.pop(0))
    assert not downs
    for j, up in enumerate(ups):
        out += EXTRAS.get((s, U + j), [])
        if j == 3:
            out += maxima + [("maxT", s + 1) if s < 3 else ("maxT0", 0)]
            maxima = []
        out.append(up)
        if j < 2:
            out += maxima[:2]
            maxima = maxima[2:]
        if j >= 1:
            out.append(("gated", up[1] - 1))
        if j >= 3:
            out.append(("pv", s * TT + j - 3))
    out.append(("gated", ups[-1][1]))
    out += [("pv", s * TT + kc) for kc in range(len(ups) - 3, TT)]
    return out


ORDER = [(s, item) for s in range(G) for item in slot_order(s)]
V_KINDS = ("max", "max0", "maxT", "maxT0", "oT", "wo", "v", "logit", "gateT")
R_KINDS = ("exp", "onT", "h1T", "qk", "h2T", "up")
NV, NRB = 2, 3
PER = {"max": 64, "maxT": 4, "exp": 64, "oT": 4, "onT": 2, "wo": 2, "v": 2, "logit": 1, "gateT": 1,
       "h1T": 2, "qk": 4, "h2T": 2, "up": NEX, "pv": 4, "down": NEX * TT}


def true_item(item):
    kind, n = item
    if kind in ("max0", "maxT0"):
        return kind[:-1], n, 1
    if kind in ("h1T", "qk", "v", "stats1", "rows1"):
        return kind, n, 1
    if kind == "up" or kind == "gated":
        return kind, n, -1 if SET_OF[n] < 2 else -2
    if kind == "down":
        return kind, n, -1 if SET_OF[n // TT] < 1 else -2
    if kind == "final":
        return kind, n, -2
    return kind, n, 0 if kind in ("max", "maxT", "exp", "pv") else -1


def ring(kinds, banks):
    seq = [item for _, item in ORDER if item[0] in kinds]
    seq += [None] * (-len(seq) % banks)
    found = {}
    for j, item in enumerate(seq):
        users = [(seq[(j - banks * r) % len(seq)], (j - banks * r) // len(seq)) for r in range(1, 60)]
        users = [user for user in users if user[0]]
        found[item] = (j % banks, users)
    return found


RINGS = {**ring(V_KINDS, NV), **ring(R_KINDS, NRB)}


def exists(b):
    return not isinstance(b, int) or 0 <= b < B


def is_at(i, n):
    return isinstance(i, int) and i == n


def wait(eng, sem, per, b, k):
    value = b * per + k
    if isinstance(value, int) and value <= 0:
        return
    eng.wait_ge(sem, value)


def block_kernel(nc, x, c_t, wmod, wqkvo, bqk_in, bv, bo, w_up, w_down, router, out):
    q_d = nc.dram_tensor("q_parts", (2, DC, P, S), F16, kind="Internal").ap()
    k_d = nc.dram_tensor("k_parts", (2, DC, P, S), F16, kind="Internal").ap()
    gmod_d = nc.dram_tensor("gate_mods", (B, 2 * D), F32, kind="Internal").ap()
    tmod_d = nc.dram_tensor("feature_mods", (B, P, 8), F32, kind="Internal").ap()
    gate_d = nc.dram_tensor("gates_by_expert", (NR, S), F32, kind="Internal").ap()

    ctx = ExitStack()
    with ctx:
        def sb(name, shape, dt=F32):
            return ctx.enter_context(nc.sbuf_tensor(name, shape, dt))

        def sem(name):
            return ctx.enter_context(nc.semaphore(name))

        ident = sb("ident", [P, P])
        ident16 = sb("ident16", [P, P], F16)
        expert_no = sb("expert_no", [P, NR], I32)
        minus_half = sb("minus_half", [P, TT])
        w4 = [sb(f"wqkvo_{n}", [P, 4, DC, D], F16) for n in ("hi", "lo")]
        wr = [sb(f"router_{n}", [P, DC, NR], F16) for n in ("hi", "lo")]
        wu = [sb(f"up_{n}", [P, DC, NEX * E], F16) for n in ("hi", "lo")]
        wd = [sb(f"down_{n}", [P, NEX, D], F16) for n in ("hi", "lo")]
        bqk = sb("bqk", [P, 4])
        bv_all = sb("bv_all", [P, D])
        bo_all = sb("bo_all", [P, D])
        mod_pre = sb("mod_pre", [P, 8])
        mod_post = sb("mod_post", [P, 8])
        ga_all, gb_all = sb("ga_all", [P, 1, D]), sb("gb_all", [P, 1, D])
        x_pre = sb("x_pre", [P, TT, D])
        x_post2 = [sb(f"x_post{b}", [P, TT, D]) for b in range(2)]
        rows = sb("rows", [P, TT, D])
        f_ring = sb("f_ring", [P, 2, S])
        h1 = [sb(f"h1_{n}", [P, DC, S], F16) for n in ("hi", "lo")]
        qk = [sb(f"qk_{n}", [P, 2, S], F16) for n in ("hi", "lo")]
        z2 = [[sb(f"z{b}_{n}", [P, DC, S], F16) for n in ("hi", "lo")] for b in range(2)]
        q_aug = [sb(f"q_aug{n}", [P, H // 2, S], F16) for n in range(2)]
        k_aug = [sb(f"k_aug{n}", [P, H // 2, S], F16) for n in range(2)]
        v_aug = [sb(f"v_aug{n}", [P, TT, H * VW + P // 4 - VW]) for n in range(2)]
        neg_max = sb("neg_max", [P, 2, TT, P], F16)
        probs = sb("probs", [P, U, S])
        o_raw = sb("o_raw", [P, G, S])
        act = [sb(f"act_{n}", [P, SETLEN, S], F16) for n in ("hi", "lo")]
        gelu = sb("gelu", [P, 4, S])
        gates = sb("gates", [P, 8, S])
        gate_rows = sb("gate_rows", [NR, S])
        stats = sb("stats", [P, TT, 6])
        mv = [sb(f"mean_var{n}", [P, TT, 2]) for n in range(2)]
        rstd = [sb(f"rstd{n}", [P, TT]) for n in range(2)]
        rsum = sb("rsum", [P, TT, H])
        logits = sb("logits", [P, TT, NR])
        top8 = sb("top8", [P, TT, 8])
        idx8 = sb("idx8", [P, TT, 8], U32)
        hit = sb("hit", [P, TT, TOPK, NR])
        ga_bo = hit[:].rearrange("p t k e -> p (t k e)")
        chosen = sb("chosen", [P, TT, NR])
        shifted = sb("shifted", [P, TT, NR])
        e16 = sb("e16", [P, TT, NR])
        esum = sb("esum", [P, TT])
        zero_row = sb("zero_row", [1, S // 2], F16)

        wmod_st = probs[:, 0:6, :].rearrange("p a n -> p (a n)").rearrange("p (c n) -> p c n", c=DC)
        w4_st = o_raw[:, :, :].rearrange("p (w c) (a n) -> p (w c a) n", w=4, n=D)
        w_st = gates[:, :, :].rearrange("p a n -> p (a n)")[:, 0:NST * WL].rearrange("p (k n) -> p k n", k=NST)
        silu = probs[:, 6, 0:DC * B].rearrange("p (c b) -> p c b", c=DC)
        silu_t = probs[:, 7, 0:DC * B].rearrange("p (c b) -> p c b", c=DC)
        ct_st = probs[:, 8, 0:DC * B].rearrange("p (c b) -> p c b", c=DC)
        wr_st = probs[:, 9, 0:DC * NR].rearrange("p (c n) -> p c n", c=DC)
        tmod_st = probs[:, 10, 0:8 * B].rearrange("p (b k) -> p b k", b=B)
        gm = [probs[0:B, 11 + n, 0:2 * D] for n in range(3)]

        VB = [ctx.enter_context(nc.psum_tensor(f"vector_bank{n}", [P, S], F32)) for n in range(NV)]
        RB = [ctx.enter_context(nc.psum_tensor(f"scalar_bank{n}", [P, S], F32)) for n in range(NRB)]
        OB = ctx.enter_context(nc.psum_tensor("pv_bank", [P, S], F32))
        DB = [ctx.enter_context(nc.psum_tensor(f"down_bank{n}", [P, S], F32)) for n in range(2)]

        def piece(parts, n):
            part = parts[n // (NW // 2)]
            flat = part[:].rearrange("p a n -> p (a n)")
            n = n % (NW // 2)
            return flat[:, WL * n:WL * (n + 1)]

        made = {k: sem(f"made_{k}") for k in PER}
        taken = {k: sem(f"taken_{k}") for k in PER}
        s_const = sem("constants_ready")
        s_passed = sem("waits_passed")
        s_w4, s_mod_in, s_small = sem("w4_loaded"), sem("mod_loaded"), sem("biases_loaded")
        s_w4s, s_silu, s_setup_mm, s_setup_v = sem("w4_split"), sem("silu_steps"), sem("mods_made"), sem("setup_vector")
        s_gm_st = sem("mods_stored")
        s_wst = [sem(f"expert_weights_staged{n}") for n in range(NST)]
        s_whi, s_wlo = sem("expert_weights_hi"), sem("expert_weights_lo")
        s_ct, s_mod0, s_drain = sem("c_loaded"), sem("first_mods_made"), sem("gated_in_drain")
        s_xpre, s_mpre = sem("x_pre_loaded"), sem("mod_pre_loaded")
        s_xpost, s_mpost = sem("x_post_loaded"), sem("mod_post_loaded")
        s_ga, s_gb = sem("ga_loaded"), sem("gb_loaded")
        s_ln1, s_ln2 = sem("ln1_steps"), sem("ln2_steps")
        s_rs1, s_rs2 = sem("rstd1_steps"), sem("rstd2_steps")
        s_onlo, s_h1lo, s_qklo, s_h2lo = sem("attention_lo"), sem("h1_lo"), sem("qk_lo"), sem("h2_lo")
        s_qkst, s_aug = [sem("qk0_stored"), sem("qk1_stored")], sem("score_operands_loaded")
        s_xg = sem("residual_plus_gated_bias")
        s_on = sem("normalised_steps")
        s_x2 = sem("attention_added")
        s_top, s_e16 = sem("router_steps"), sem("router_exp")
        s_gst, s_gld = sem("gates_stored"), [sem("gates0_loaded"), sem("gates1_loaded")]
        s_ehi, s_gated, s_elo = sem("expert_hi_made"), sem("expert_gated"), sem("expert_lo_made")
        s_fin, s_sum, s_out = sem("experts_times_gb"), sem("experts_added"), sem("out_stored")
        s_aug0 = sem("score_operand_constants")

        def wait_apart(eng, sem, per, b, k):
            wait(eng, sem, per, b, k)
            if not isinstance(b, int):
                eng.sem_inc(s_passed, 1)

        block = ctx.enter_context(nc.Block())

        def bank(item):
            kind = item[0]
            n = RINGS[item][0]
            return (VB if kind in V_KINDS else RB)[n]

        def wait_bank(eng, item, i):
            for prev, back in RINGS[item][1]:
                kind, n, lag = true_item(prev)
                b = i + back + lag
                if exists(b) or (not isinstance(i, int)):
                    wait(eng, taken[kind], PER[kind], b, n + 1)
                    return

        def iterations(eng, body):
            for i in (-1, 0, 1, 2):
                body(i, i % 2)
            with eng.Fori(0, 2) as j:
                body(j * 2 + 3, 1)
                body(j * 2 + 4, 0)
            for i in (7, 8, 9):
                body(i, i % 2)

        def items(i, s):
            for item in slot_order(s):
                kind, n, lag = true_item(item)
                if kind == "wsplit":
                    at = [a for a, piece in WSPLIT.items() if piece == n][0]
                    if is_at(i, at[0]):
                        yield item, kind, n, i
                elif exists(i + lag):
                    yield item, kind, n, i + lag


        @block.sync
        def _(sp):
            def stage(n):
                if n >= NST:
                    sp.wait_ge(s_wlo, n - NST + 1)
                src = w_up[P * (n // 2):P * (n // 2 + 1), WL * (n % 2):WL * (n % 2 + 1)] if n < NW // 2 else \
                    w_down[:, WL * (n - NW // 2):WL * (n - NW // 2 + 1)]
                sp.dma_start(w_st[:, n % NST, :], src).then_inc(s_wst[n % NST], 16)

            sp.dma_start(ct_st, c_t.rearrange("(c p) b -> p c b", c=DC)).then_inc(s_ct, 16)
            sp.dma_start(x_pre[:], x[0].rearrange("(t p) d -> p t d", t=TT)).then_inc(s_xpre, 16)
            sp.dma_start(wmod_st, wmod.rearrange("(c p) n -> p c n", c=DC)).then_inc(s_mod_in, 16)
            for w in range(4):
                sp.dma_start(w4_st[:, 2 * w:2 * w + 2, :], wqkvo[w].rearrange("(c p) n -> p c n", c=DC)).then_inc(s_w4, 16)
            sp.dma_start(bqk[:], bqk_in).then_inc(s_small, 16)
            sp.dma_start(bv_all[:], bv.partition_broadcast(P)).then_inc(s_small, 16)
            sp.dma_start(bo_all[:], bo.partition_broadcast(P)).then_inc(s_small, 16)
            sp.dma_start(wr_st, router.rearrange("(c p) n -> p c n", c=DC)).then_inc(s_small, 16)
            for n in range(NST):
                stage(n)
            sp.wait_ge(s_setup_v, 8)
            sp.dma_start(tmod_d.rearrange("b p k -> p b k"), tmod_st).then_inc(s_gm_st, 16)
            sp.dma_start(gmod_d, gm[2]).then_inc(s_gm_st, 16)
            sp.wait_ge(s_aug0, 6)

            def body(i, par):
                b = i + 1
                if is_at(i, 0):
                    sp.wait_ge(s_gm_st, 32)
                    for n in (6, 7):
                        stage(n)
                if exists(b) and not is_at(i, -1):
                    wait_apart(sp, s_ln1, 12, b, 0)
                    sp.dma_start(x_pre[:], x[b].rearrange("(t p) d -> p t d", t=TT)).then_inc(s_xpre, 16)
                    wait_apart(sp, taken["h1T"], 2, b, 0)
                    sp.dma_start(mod_pre[:], tmod_d[b]).then_inc(s_mpre, 16)
                b = i + 1
                if exists(b):
                    qa, ka = q_aug[1 - par], k_aug[1 - par]
                    for n in range(4):
                        dst = (q_d, k_d)[n // 2]
                        wait_apart(sp, s_qklo, 4, b, n + 1)
                        if n == 0:
                            wait_apart(sp, s_aug, 16 * 14, b, 0)
                        for part in range(2):
                            sp.dma_start(dst[part, n % 2], qk[part][:, n % 2, :]).then_inc(s_qkst[n % 2], 16)
                        if n % 2 == 1:
                            for m in range(2):
                                wait_apart(sp, s_qkst[m], 64, b, 32 * (n // 2 + 1))
                            if n == 1:
                                wait_apart(sp, made["exp"], 64, i, 0)
                                wait_apart(sp, made["max"], 64, i, 0)
                            aug = (qa, ka)[n // 2]
                            for par2 in range(2):
                                for row, part in ((0, 0), (16, n // 2 == 0), (48, n // 2)):
                                    src = dst[int(part)].rearrange("c (p two d) t -> two d (c p) t", two=2, d=DH)[par2]
                                    at = 64 * par2 + row
                                    sp.dma_start(aug[at:at + DH, :, :], src).then_inc(s_aug, 16)
                    for par2 in range(2):
                        sp.dma_start(qa[64 * par2 + 32:64 * par2 + 33, :, :].rearrange("r a (b n) -> r (a b) n", b=2),
                                     zero_row[0:1, :].unsqueeze(1).broadcast_to([1, H, S // 2])).then_inc(s_aug, 16)
                b = i - 1
                if is_at(i, -1):
                    for n in (3, 4, 5):
                        stage(n)
                if exists(b):
                    wait_apart(sp, taken["gateT"], 1, b, 1)
                    for m in range(2):
                        wait_apart(sp, s_gld[m], 32, b, 0)
                    sp.dma_start(gate_d, gate_rows[:, :]).then_inc(s_gst, 16)
                    wait_apart(sp, s_gst, 16, b, 16)
                for quarter in range(4):
                    if quarter == 2 and exists(i - 2):
                        wait_apart(sp, s_sum, 2, i - 2, 2)
                        sp.dma_start(out[i - 2].rearrange("(t p) d -> p t d", t=TT), x_post2[par][:]).then_inc(s_out, 16)
                    if quarter == 2 and exists(b):
                        wait_apart(sp, s_fin, 2, b, 0)
                        sp.dma_start(gb_all[:, 0, :], gmod_d[b, D:2 * D].partition_broadcast(P)).then_inc(s_gb, 16)
                    if quarter == 2 and exists(i):
                        wait_apart(sp, taken["wo"], 2, i, 0)
                        sp.dma_start(ga_all[:, 0, :], gmod_d[i, 0:D].partition_broadcast(P)).then_inc(s_ga, 16)
                        wait_apart(sp, taken["h2T"], 2, i, 0)
                        sp.dma_start(mod_post[:], tmod_d[i]).then_inc(s_mpost, 16)
                        wait_apart(sp, s_out, 16, i - 1, 0)
                        sp.dma_start(x_post2[par][:], x[i].rearrange("(t p) d -> p t d", t=TT)).then_inc(s_xpost, 16)
                    if exists(b):
                        wait_apart(sp, s_elo, NEX, b, NSH + 4 * quarter + 4 - 8 - (NSH if quarter < 2 else 0))
                        at = 4 * (quarter % 2)
                        sp.dma_start(gates[:, at:at + 4, :], gate_d[4 * quarter:4 * quarter + 4, :].partition_broadcast(P)
                                     ).then_inc(s_gld[quarter % 2], 16)

            iterations(sp, body)
            sp.wait_ge(s_out, 16 * B)
            sp.wait_ge(s_gst, 16 * B)
            for m in range(2):
                sp.wait_ge(s_qkst[m], 64 * B)

        @block.gpsimd
        def _(pool):
            pool.memset(minus_half[:], -0.5).then_inc(s_const, 1)
            pool.memset(ident[:], 0.0).then_inc(s_const, 1)
            pool.memset(ident16[:], 0.0).then_inc(s_const, 1)
            pool.iota(expert_no[:], [[1, NR]], base=0, channel_multiplier=0).then_inc(s_const, 1)
            pool.wait_ge(s_const, 4)
            for m in (ident, ident16):
                pool.affine_select(out=m[:], in_=m[:], compare_op=ALU.not_equal, fill=1.0, base=0,
                                   pattern=[[-1, P]], channel_multiplier=1).then_inc(s_const, 1)
            pool.memset(neg_max[:], 0.0).then_inc(s_const, 1)
            pool.memset(zero_row[:], 0.0).then_inc(s_const, 1)
            def power(b, m, r, s_stats, s_rs):
                wait_apart(pool, s_stats, 12, b, 8)
                pool.tensor_scalar(r[:], m[:, :, 1], EPS, None, ALU.add).then_inc(s_rs, 1)
                wait(pool, s_rs, 2, b, 1)
                pool.tensor_tensor(r[:], r[:], minus_half[:], ALU.pow).then_inc(s_rs, 1)

            power(0, mv[0], rstd[0], s_ln1, s_rs1)
            for n in (1, 0):
                pool.memset(q_aug[n][:].bitcast(U32), 0).then_inc(s_aug0, 1)
                pool.memset(k_aug[n][:].bitcast(U32), 0x3C003C00).then_inc(s_aug0, 1)
                pool.memset(v_aug[n][:], 1.0).then_inc(s_aug0, 1)

            def lo_part(kind, n, b, hi, lo, s_lo):
                wait(pool, taken[kind], PER[kind], b, n + 1)
                pool.tensor_tensor(lo, f_ring[:, n % 2, :], hi, ALU.subtract).then_inc(s_lo, 1)

            def body(i, par):
                drain = isinstance(i, int) and i >= B
                z = z2[1 - par]
                b = i - 1
                if exists(b):
                    x_post = x_post2[1 - par]
                    wait(pool, s_ga, 16, b, 16)
                    wait(pool, s_top, 15, b, 0)
                    pool.tensor_tensor(ga_bo, ga_all[:, 0, :], bo_all[:], ALU.mult).then_inc(s_xg, 1)
                    wait(pool, s_xg, 2, b, 1)
                    wait(pool, s_xpost, 16, b, 16)
                    pool.tensor_tensor(x_post[:], x_post[:], ga_bo.unsqueeze(1).broadcast_to([P, TT, D]), ALU.add).then_inc(s_xg, 1)
                for s in range(G):
                    for item, kind, n, b in items(i, s):
                        if kind == "wsplit":
                            pool.wait_ge(s_whi, n + 1)
                            pool.tensor_tensor(piece((wu[1], wd[1]), n), w_st[:, n % NST, :], piece((wu[0], wd[0]), n),
                                               ALU.subtract).then_inc(s_wlo, 1)
                        elif kind == "stats1" and not is_at(i, -1):
                            power(b, mv[0], rstd[0], s_ln1, s_rs1)
                        elif kind == "stats2":
                            power(b, mv[1], rstd[1], s_ln2, s_rs2)
                        if kind == "h1T":
                            if n == 0:
                                wait(pool, made["v"], 2, b, 0)
                            lo_part(kind, n, b, h1[0][:, n, :], h1[1][:, n, :], s_h1lo)
                        elif kind == "qk":
                            lo_part(kind, n, b, qk[0][:, n % 2, :], qk[1][:, n % 2, :], s_qklo)
                        elif kind == "h2T":
                            lo_part(kind, n, b, z[0][:, n, :], z[1][:, n, :], s_h2lo)
                        elif kind == "onT":
                            lo_part(kind, n, b, z[0][:, n, :], z[1][:, n, :], s_onlo)
                        elif kind == "wo":
                            wait(pool, taken["wo"], 2, b, n + 1)
                            wait_apart(pool, s_xg, 2, b, 2)
                            xs = x_post2[1 - par][:, 2 * n:2 * n + 2, :]
                            pool.tensor_tensor(xs, xs, rows[:, 2 * n:2 * n + 2, :], ALU.add).then_inc(s_x2, 1)
                        elif kind == "final":
                            for m in range(2):
                                wait(pool, s_fin, 2, b, m + 1)
                                xs = x_post2[par][:, 2 * m:2 * m + 2, :]
                                pool.tensor_tensor(xs, xs, rows[:, 2 * m:2 * m + 2, :], ALU.add).then_inc(s_sum, 1)
                        elif kind == "gated":
                            c = n - SETS[SET_OF[n]]
                            wait(pool, s_ehi, NEX, b, n + 1)
                            if n >= NSH and not drain:
                                g = gelu[:, n % 4, :]
                                pool.tensor_tensor(g, g, gates[:, (n - NSH) % 8, :], ALU.mult).then_inc(s_gated, 1)
                                wait(pool, s_gated, NR, b, n - NSH + 1)
                            pool.tensor_tensor(act[1][:, c, :], gelu[:, n % 4, :], act[0][:, c, :],
                                               ALU.subtract).then_inc(s_elo, 1)
            iterations(pool, body)

        @block.scalar
        def _(scalar):
            scalar.wait_ge(s_ct, 16)
            scalar.activation(silu_t, ct_st, ACT.Exp, scale=-1.0).then_inc(s_silu, 1)
            scalar.wait_ge(s_small, 64)

            def split_out(kind, n, b, src, hi, f, scale, bias):
                scalar.activation(hi, src, ACT.Identity, bias=bias, scale=scale)
                scalar.activation(f, src, ACT.Identity, bias=bias, scale=scale).then_inc(taken[kind], 1)

            def body(i, par):
                for s in range(G):
                    for item, kind, n, b in items(i, s):
                        if kind == "e16":
                            wait(scalar, s_top, 15, b, 9)
                            scalar.activation(e16[:], shifted[:], ACT.Exp).then_inc(s_e16, 1)
                        if kind == "wsplit":
                            scalar.wait_ge(s_wst[n % NST], 16 * (n // NST + 1))
                            scalar.activation(piece((wu[0], wd[0]), n), w_st[:, n % NST, :], ACT.Copy).then_inc(s_whi, 1)
                        if item[0] not in R_KINDS:
                            continue
                        src = bank(item)
                        wait(scalar, made[kind], PER[kind], b, n + 1)
                        if kind == "exp":
                            if n % U == 0:
                                wait(scalar, made["pv"], 4, b, n // U)
                            scalar.activation(probs[:, n % U, :], src[:], ACT.Exp, scale=SCALE).then_inc(taken[kind], 1)
                        elif kind == "h1T":
                            if n == 0:
                                if is_at(i, -1):
                                    scalar.wait_ge(s_mod0, 2)
                                wait(scalar, s_mpre, 16, b, 0)
                                wait(scalar, made["v"], 2, b, 0)
                            if exists(i - 1):
                                wait(scalar, s_h2lo, 2, i - 1, n + 1)
                            else:
                                wait(scalar, s_qklo, 4, b, 0)
                            split_out(kind, n, b, src[:], h1[0][:, n, :], f_ring[:, n, :],
                                      mod_pre[:, 2 + n:3 + n], mod_pre[:, n:n + 1])
                        elif kind == "qk":
                            if n < 2:
                                wait(scalar, s_h1lo, 2, b, 2)
                                wait(scalar, s_qkst[n], 64, b, 0)
                            else:
                                wait(scalar, s_qklo, 4, b, n - 1)
                                wait(scalar, s_qkst[n - 2], 64, b, 32)
                            scalar.activation(qk[0][:, n % 2, :], src[:], ACT.Identity, bias=bqk[:, n:n + 1])
                            scalar.activation(f_ring[:, n % 2, :], src[:], ACT.Identity, bias=bqk[:, n:n + 1]).then_inc(taken[kind], 1)
                        elif kind == "onT":
                            z = z2[1 - par]
                            wait(scalar, s_qklo, 4, min(i, B - 1) if isinstance(i, int) else i, 4)
                            wait(scalar, made["up"], NEX, b - 1, 0)
                            wait(scalar, made["logit"], 1, b - 1, 0)
                            scalar.activation(z[0][:, n, :], src[:], ACT.Copy)
                            scalar.activation(f_ring[:, n, :], src[:], ACT.Copy).then_inc(taken[kind], 1)
                        elif kind == "h2T":
                            if n == 0:
                                wait(scalar, s_mpost, 16, b, 16)
                            z = z2[1 - par]
                            wait(scalar, s_onlo, 2, b, n + 1)
                            wait(scalar, made["wo"], 2, b, 2)
                            split_out(kind, n, b, src[:], z[0][:, n, :], f_ring[:, n, :],
                                      mod_post[:, 6 + n:7 + n], mod_post[:, 4 + n:5 + n])
                        elif kind == "up":
                            wait(scalar, s_elo, NEX, b, max(n - 3, 0))
                            scalar.activation(gelu[:, n % 4, :], src[:], ACT.Gelu).then_inc(taken[kind], 1)

            iterations(scalar, body)

        @block.vector
        def _(dve):
            def ln_stats(src, m, s_ln, b, ready, per, k):
                for t in range(TT):
                    if t == 0:
                        wait(dve, ready, per, b, k)
                    dve.bn_stats(stats[:, t, :], src[:, t, :]).then_inc(s_ln, 1)
                for t in range(TT):
                    if t == 0:
                        wait_apart(dve, s_ln, 12, b, 4)
                    dve.bn_aggr(m[:, t, :], stats[:, t, :]).then_inc(s_ln, 1)

            def ln_rows(src, m, r, s_ln, s_rs, b):
                wait(dve, s_rs, 2, b, 2)
                for t in range(TT):
                    dve.tensor_scalar(rows[:, t, :], src[:, t, :], m[:, t, 0:1], r[:, t:t + 1],
                                      ALU.subtract, ALU.mult).then_inc(s_ln, 1)

            dve.wait_ge(s_silu, 1)
            dve.tensor_scalar(silu_t, silu_t, 1.0, None, ALU.add).then_inc(s_silu, 1)
            dve.wait_ge(s_silu, 2)
            dve.reciprocal(silu_t, silu_t).then_inc(s_silu, 1)
            dve.wait_ge(s_silu, 3)
            dve.tensor_tensor(silu, silu_t, ct_st, ALU.mult).then_inc(s_silu, 1)
            ln_stats(x_pre, mv[0], s_ln1, 0, s_xpre, 16, 16)
            ln_rows(x_pre, mv[0], rstd[0], s_ln1, s_rs1, 0)
            w4f = w4_st.rearrange("p a n -> p (a n)")
            hi4, lo4 = (w[:].rearrange("p w c n -> p (w c n)") for w in w4)
            dve.wait_ge(s_w4, 64)
            dve.tensor_copy(hi4, w4f).then_inc(s_w4s, 1)
            dve.wait_ge(s_w4s, 1)
            dve.tensor_tensor(lo4, w4f, hi4, ALU.subtract).then_inc(s_w4s, 1)
            src, src2 = (m[:, 0:8 * B].rearrange("p (k b) -> p b k", k=8) for m in (DB[0], OB))
            dve.wait_ge(s_setup_mm, 1)
            for n, add in ((0, 0.0), (2, 1.0)):
                dve.tensor_scalar(mod_pre[:, n:n + 2], src[:, 0, n:n + 2], add, None, ALU.add).then_inc(s_mod0, 1)
            dve.wait_ge(s_setup_mm, 2)
            for n, add in ((0, 0.0), (2, 1.0), (4, 0.0), (6, 1.0)):
                dve.tensor_scalar(tmod_st[:, :, n:n + 2], (src if n < 4 else src2)[:, :, n:n + 2], add, None, ALU.add).then_inc(s_setup_v, 1)
            g = DB[1][0:B, 0:2 * D]
            dve.tensor_scalar(gm[0], g, 0.0, 2.0, ALU.is_ge, ALU.mult).then_inc(s_setup_v, 1)
            dve.tensor_scalar(gm[1], g, -1.0, MINGATE, ALU.mult, ALU.max).then_inc(s_setup_v, 1)
            dve.wait_ge(s_setup_v, 6)
            dve.tensor_tensor(gm[1], gm[1], g, ALU.max).then_inc(s_setup_v, 1)
            dve.wait_ge(s_setup_v, 7)
            dve.scalar_tensor_tensor(gm[2], gm[0], -1.0, gm[1], ALU.add, ALU.mult).then_inc(s_setup_v, 1)
            dve.wait_ge(s_small, 64)
            dve.tensor_copy(wr[0][:], wr_st).then_inc(s_setup_v, 1)
            dve.wait_ge(s_setup_v, 9)
            dve.tensor_tensor(wr[1][:], wr_st, wr[0][:], ALU.subtract).then_inc(s_setup_v, 1)

            drained = [0]

            def top_four(b):
                w = lambda k: wait_apart(dve, s_top, 15, b, k)
                wait_apart(dve, taken["logit"], 1, b, 1)
                for t in range(TT):
                    dve.max(top8[:, t, :], logits[:, t, :]).then_inc(s_top, 1)
                w(4)
                for t in range(TT):
                    dve.max_index(idx8[:, t, :], top8[:, t, :], logits[:, t, :]).then_inc(s_top, 1)
                dve.tensor_tensor(shifted[:], logits[:], top8[:, :, 0:1].broadcast_to([P, TT, NR]),
                                  ALU.subtract).then_inc(s_top, 1)
                w(8)
                dve.tensor_tensor(hit[:], idx8[:, :, 0:TOPK].unsqueeze(3).broadcast_to([P, TT, TOPK, NR]),
                                  expert_no[:].unsqueeze(1).unsqueeze(1).broadcast_to([P, TT, TOPK, NR]),
                                  ALU.is_equal).then_inc(s_top, 1)
                w(10)
                dve.tensor_reduce(chosen[:], hit[:].rearrange("p t k e -> p t e k"), AX.X, ALU.add).then_inc(s_top, 1)

            def gate_values(b):
                w = lambda k: wait_apart(dve, s_top, 15, b, k)
                wait(dve, s_e16, 1, b, 1)
                dve.tensor_reduce(esum[:], e16[:], AX.X, ALU.add).then_inc(s_top, 1)
                w(12)
                dve.reciprocal(esum[:], esum[:]).then_inc(s_top, 1)
                w(11)
                dve.tensor_tensor(chosen[:], chosen[:], e16[:], ALU.mult).then_inc(s_top, 1)
                w(14)
                dve.tensor_tensor(chosen[:], chosen[:], esum[:].unsqueeze(2).broadcast_to([P, TT, NR]),
                                  ALU.mult).then_inc(s_top, 1)

            def body(i, par):
                nb, pb = i + 1, i - 1
                x_post, z = x_post2[1 - par], z2[1 - par]
                for s in range(G):
                    for item, kind, n, b in items(i, s):
                        if kind == "stats1" and not is_at(i, -1):
                            if exists(pb):
                                wait(dve, s_ln2, 12, pb - 1, 8)
                            ln_stats(x_pre, mv[0], s_ln1, nb, s_xpre, 16, 16)
                        if kind == "rows1" and not is_at(i, -1):
                            if exists(pb):
                                wait(dve, made["h2T"], 2, pb, 2)
                            ln_rows(x_pre, mv[0], rstd[0], s_ln1, s_rs1, nb)
                        if kind == "top":
                            top_four(b)
                        if kind == "gates":
                            gate_values(b)
                        if kind == "final":
                            wait(dve, s_gb, 16, b, 16)
                            wait(dve, made["down"], NEX * TT, b, NEX * TT)
                            for m in range(2):
                                dve.tensor_tensor(rows[:, 2 * m:2 * m + 2, :], DB[m][:].rearrange("p (t d) -> p t d", t=2),
                                                  gb_all[:, 0:1, :].broadcast_to([P, 2, D]), ALU.mult).then_inc(s_fin, 1)
                        if kind == "stats2":
                            wait(dve, s_ln1, 12, min(nb, B - 1) if isinstance(nb, int) else nb, 8)
                            ln_stats(x_post, mv[1], s_ln2, b, s_x2, 2, 2)
                        if kind == "rows2":
                            ln_rows(x_post, mv[1], rstd[1], s_ln2, s_rs2, pb)
                        if kind == "gated":
                            g = gelu[:, n % 4, :]
                            wait(dve, taken["up"], NEX, b, n + 1)
                            c = n - SETS[SET_OF[n]]
                            if c == 0:
                                wait(dve, made["down"], NEX * TT, b, n * TT)
                            if n < NSH:
                                dve.tensor_copy(act[0][:, c, :], g).then_inc(s_ehi, 1)
                            else:
                                quarter, rest = divmod(n - NSH, 4)
                                if rest == 0:
                                    wait(dve, s_gld[quarter % 2], 32, b, 16 * (quarter // 2 + 1))
                                if isinstance(i, int) and i >= B:
                                    dve.tensor_tensor(g, g, gates[:, (n - NSH) % 8, :], ALU.mult).then_inc(s_drain, 1)
                                    drained[0] += 1
                                    dve.wait_ge(s_drain, drained[0])
                                    dve.tensor_copy(act[0][:, c, :], g).then_inc(s_ehi, 1)
                                else:
                                    dve.tensor_tensor(act[0][:, c, :], g, gates[:, (n - NSH) % 8, :], ALU.mult).then_inc(s_ehi, 1)
                        if item[0] not in V_KINDS:
                            continue
                        src = bank(item)
                        wait(dve, made[kind], PER[kind], b, n + 1)
                        done = taken[kind]
                        if kind == "max":
                            u = n % U
                            dve.tensor_reduce(neg_max[:, u // 8, (u // 2) % TT, 32 + 64 * (u % 2):33 + 64 * (u % 2)],
                                              src[:], AX.X, ALU.max, negate=True).then_inc(done, 1)
                        elif kind == "maxT":
                            qa = q_aug[par if b is i or n else 1 - par]
                            if item[0] == "maxT0":
                                qa = q_aug[1 - par]
                            srcT = src[:].bitcast(F16).rearrange("p (a n) -> p a n", a=2)
                            dve.tensor_copy(qa[32:33, 2 * n:2 * n + 2, :], srcT[32:33, :, :])
                            dve.tensor_copy(qa[96:97, 2 * n:2 * n + 2, :], srcT[96:97, :, :]).then_inc(done, 1)
                        elif kind == "oT":
                            o = src[:].rearrange("p (h w) -> p h w", h=H)
                            if n == 0 and exists(i):
                                wait(dve, made["h1T"], 2, i, 2)
                            if n == 0:
                                wait(dve, s_sum, 2, b - 1, 0)
                            dve.reciprocal(rsum[:, n, :], o[:, :, 0]).then_inc(s_on, 1)
                            wait(dve, s_on, 4, b, n + 1)
                            dve.tensor_tensor(rows[:, n, :].rearrange("p (h w) -> p h w", h=H), o[:, :, 1:VW],
                                              rsum[:, n, :].unsqueeze(2).broadcast_to([P, H, DH]), ALU.mult).then_inc(done, 1)
                        elif kind == "wo":
                            if n == 0:
                                wait(dve, s_ga, 16, b, 16)
                            dve.tensor_tensor(rows[:, 2 * n:2 * n + 2, :], src[:].rearrange("p (t d) -> p t d", t=2),
                                              ga_all[:, 0:1, :].broadcast_to([P, 2, D]), ALU.mult).then_inc(done, 1)
                        elif kind == "v":
                            va = v_aug[1 - par]
                            if n == 0:
                                dve.wait_ge(s_aug0, 6)
                                wait(dve, made["pv"], 4, i, 0)
                            for t in range(2):
                                ins = dve.tensor_tensor(
                                    va[:, 2 * n + t, 0:H * VW].rearrange("p (h w) -> p h w", h=H)[:, :, 1:VW],
                                    src[:, t * D:(t + 1) * D].rearrange("p (h w) -> p h w", h=H),
                                    bv_all[:].rearrange("p (h w) -> p h w", h=H), ALU.add)
                            ins.then_inc(done, 1)
                        elif kind == "logit":
                            dve.tensor_copy(logits[:].rearrange("p t e -> p (t e)"), src[:, 0:TT * NR]).then_inc(done, 1)
                        elif kind == "gateT":
                            wait(dve, s_gst, 16, b, 0)
                            dve.tensor_copy(gate_rows[:, :], src[0:NR, :]).then_inc(done, 1)
                    if exists(i):
                        wait(dve, made["pv"], 4, i, s + 1)
                        wait(dve, made["oT"], 4, i, 0)
                        dve.tensor_copy(o_raw[:, s, :], OB[:]).then_inc(taken["pv"], 1)

            iterations(dve, body)

        @block.tensor
        def _(pe):
            def split_product(dst, pairs, last_sem=None):
                terms = [(a, b) for st, mo in pairs for a, b in ((st[0], mo[0]), (st[0], mo[1]), (st[1], mo[0]))]
                for n, (a, b) in enumerate(terms):
                    ins = pe.matmul(dst, a, b, start=n == 0, stop=n == len(terms) - 1)
                return ins

            pe.wait_ge(s_silu, 4)
            pe.wait_ge(s_mod_in, 16)
            for k, col in enumerate((0, D, 3 * D, 4 * D)):
                for half in range(2):
                    for c in range(DC):
                        o = (DB[0] if k < 2 else OB)[:, (2 * k + half) * B:(2 * k + half + 1) * B]
                        ins = pe.matmul(o, wmod_st[:, c, col + P * half:col + P * half + P], silu[:, c, :],
                                        start=c == 0, stop=c == DC - 1)
                if k == 1:
                    ins.then_inc(s_setup_mm, 1)
            for k, col in enumerate((2 * D, 5 * D)):
                for c in range(DC):
                    ins = pe.matmul(DB[1][0:B, D * k:D * k + D], silu[:, c, :], wmod_st[:, c, col:col + D],
                                    start=c == 0, stop=c == DC - 1)
            ins.then_inc(s_setup_mm, 1)
            pe.wait_ge(s_const, 8)
            pe.wait_ge(s_w4s, 2)

            def unit(n):
                u = n % U
                return (n // U) * 2 + u // 8, 64 * (u % 2), (u // 2) % TT

            def body(i, par):
                for s in range(G):
                    for item, kind, n, b in items(i, s):
                        z = z2[par if kind == "up" and SET_OF[n] >= 2 else 1 - par]
                        if kind in V_KINDS or kind in R_KINDS:
                            wait_bank(pe, item, i)
                            dst = bank(item)
                        elif kind not in PER:
                            continue
                        sig = made[kind]
                        if kind in ("max", "exp"):
                            ahead = item[0] == "max0"
                            qa, ka = q_aug[1 - par if ahead else par], k_aug[1 - par if ahead else par]
                            pair, at, t = unit(n)
                            if item == ("max0", 0):
                                wait(pe, s_aug, 16 * 14, b, 16 * 14)
                            if kind == "exp" and n % U == 0:
                                wait(pe, taken["maxT"], 4, b, n // U + 1)
                            st, mo = (qa, ka) if kind == "max" else (ka, qa)
                            pe.matmul(dst[:], st[at:at + 64, pair, t * P:(t + 1) * P], mo[at:at + 64, pair, :],
                                      start=True, stop=True).then_inc(sig, 1)
                        elif kind == "maxT":
                            wait(pe, taken["max"], PER["max"], b, U * (n + 1))
                            d16 = dst[:].bitcast(F16)
                            for a in range(2):
                                for t in range(TT):
                                    o = (a * TT + t) * P
                                    ins = pe.transpose(d16[:, o:o + P], neg_max[:, a, t, :], ident16[:])
                            ins.then_inc(sig, 1)
                        elif kind == "pv":
                            g, kc = divmod(n, TT)
                            if kc == 0:
                                if g == 0:
                                    wait(pe, taken["v"], 2, b, 2)
                                wait(pe, taken["pv"], 4, b, g)
                            if kc == 0:
                                wait(pe, taken["exp"], 64, b, U * (g + 1))
                            for j in range(GH):
                                h = g * GH + j
                                u = (j // 2) * 8 + kc * 2 + j % 2
                                ins = pe.matmul(OB[32 * j:32 * j + 32, :], v_aug[par][:, kc, h * VW:h * VW + 32],
                                                probs[:, u, :], start=kc == 0, stop=kc == TT - 1)
                            if kc == TT - 1:
                                ins.then_inc(sig, 1)
                        elif kind == "h1T" or kind == "h2T" or kind == "onT":
                            if n == 0:
                                if kind == "h1T":
                                    wait(pe, s_ln1, 12, b, 12)
                                elif kind == "h2T":
                                    wait(pe, s_ln2, 12, b, 12)
                                else:
                                    wait(pe, taken["oT"], 4, b, 4)
                            for t in range(TT):
                                ins = pe.transpose(dst[:, t * P:(t + 1) * P], rows[:, t, n * P:(n + 1) * P], ident[:])
                            ins.then_inc(sig, 1)
                        elif kind == "oT":
                            if n == 0:
                                wait(pe, taken["pv"], 4, b, 4)
                            for g in range(G):
                                ins = pe.transpose(dst[:, g * P:(g + 1) * P], o_raw[:, g, n * P:(n + 1) * P], ident[:])
                            ins.then_inc(sig, 1)
                        elif kind == "qk":
                            if n == 0:
                                wait(pe, s_h1lo, 2, b, 2)
                            w, m = divmod(n, 2)
                            split_product(dst[:], [([p[:, w, c, m * P:(m + 1) * P] for p in w4],
                                                    [p[:, c, :] for p in h1]) for c in range(DC)]).then_inc(sig, 1)
                        elif kind == "v" or kind == "wo":
                            a = h1 if kind == "v" else z
                            if n == 0 and kind == "wo":
                                wait(pe, s_onlo, 2, b, 2)
                            for t in range(2):
                                tok = (2 * n + t) * P
                                ins = split_product(dst[:, t * D:(t + 1) * D],
                                                    [([p[:, c, tok:tok + P] for p in a],
                                                      [p[:, 2 if kind == "v" else 3, c, :] for p in w4]) for c in range(DC)])
                            ins.then_inc(sig, 1)
                        elif kind == "logit":
                            wait(pe, s_h2lo, 2, b, 2)
                            for t in range(TT):
                                ins = split_product(dst[:, t * NR:(t + 1) * NR],
                                                    [([p[:, c, t * P:(t + 1) * P] for p in z],
                                                      [p[:, c, :] for p in wr]) for c in range(DC)])
                            ins.then_inc(sig, 1)
                        elif kind == "gateT":
                            wait(pe, s_top, 15, b, 15)
                            for t in range(TT):
                                ins = pe.transpose(dst[0:NR, t * P:(t + 1) * P], chosen[:, t, :], ident[:])
                            ins.then_inc(sig, 1)
                        elif kind == "up":
                            if n == 0:
                                pe.wait_ge(s_wlo, NW)
                            split_product(dst[:], [([p[:, c, n * E:(n + 1) * E] for p in wu],
                                                    [p[:, c, :] for p in z]) for c in range(DC)]).then_inc(sig, 1)
                        elif kind == "down":
                            c, t = divmod(n, TT)
                            if n == 0:
                                wait(pe, s_fin, 2, b, 0)
                            if t == 0:
                                wait(pe, s_elo, NEX, b, c + 1)
                            o = DB[t // 2][:, (t % 2) * D:(t % 2 + 1) * D]
                            for k, (a, w) in enumerate(((0, 0), (0, 1), (1, 0))):
                                ins = pe.matmul(o, act[a][:, c - SETS[SET_OF[c]], t * P:(t + 1) * P], wd[w][:, c, :],
                                                start=c == 0 and k == 0 and t % 2 == 0,
                                                stop=c == NEX - 1 and k == 2, skip_group_check=True)
                            ins.then_inc(sig, 1)

            iterations(pe, body)


def kernel(**inputs):
    import numpy as np
    import concourse.bacc as bacc
    from concourse import mybir as mb
    from concourse.bass_utils import run_bass_kernel_spmd as run

    a = {k[3:]: np.asarray(v) for k, v in inputs.items()}
    laid = {
        "x": a["attn_x"], "c_t": a["c"].T, "wmod": a["wmod"],
        "wqkvo": np.stack([a["attn_wq"], a["attn_wk"], a["attn_wv"], a["attn_wo"]]),
        "bqk": np.stack([a["attn_bq"], a["attn_bk"]]).reshape(4, P).T, "bv": a["attn_bv"], "bo": a["attn_bo"],
        "w_up": np.concatenate([a["ffn_shared_up"], a["ffn_routed_up"]]).reshape(NEX * E, D).T,
        "w_down": np.concatenate([a["ffn_shared_down"], a["ffn_routed_down"]]).transpose(2, 0, 1).reshape(E, NEX * D),
        "router": a["ffn_router_w"].T,
    }
    nc = bacc.Bacc("TRN2", target_bir_lowering=False, num_devices=1)
    arrays, args = {}, []
    for name, v in laid.items():
        v = np.ascontiguousarray(v)
        arrays[f"in_{name}"] = v
        args.append(nc.dram_tensor(f"in_{name}", v.shape, mb.dt.from_np(v.dtype), kind="ExternalInput").ap())
    out = nc.dram_tensor("out_0", (B, S, D), mb.dt.float32, kind="ExternalOutput").ap()
    block_kernel(nc, *args, out)
    r = run(nc, [arrays], core_ids=[0])
    return r.results[0]["out_0"]
```

```python
import concourse.bass as bass
from concourse import mybir
from contextlib import ExitStack

F32 = mybir.dt.float32
F16 = mybir.dt.float16
U32 = mybir.dt.uint32
I32 = mybir.dt.int32
ALU = mybir.AluOpType
ACT = mybir.ActivationFunctionType
AX = mybir.AxisListType

B, S, D = 8, 512, 256
H, DH = 16, 16
E, NSH, NEX = 128, 2, 18
NR, TOPK = NEX - NSH, 4
P = 128
TT = S // P
DC = D // P
G, GH = 4, 4
U = GH * TT
NGELU = 3
VW = DH + 1
NW, WL = 8, 2 * DC * NEX * E // 8
NST = 3
VROW = 2 * -(-(H * VW + P // 4 - VW) // 2)
EPS = 1e-5
SCALE = DH ** -0.5
MINGATE = 0.25

SETS = [0, 5, 10, 14, 18]
SETLEN = max(b - a for a, b in zip(SETS, SETS[1:]))
SET_OF = [sum(c >= e for e in SETS[1:]) for c in range(NEX)]
UP_SET = {2: 0, 3: 1, 0: 2, 1: 3}
DOWN_SET = {3: 0, 0: 1, 1: 2, 2: 3}
EXTRAS = {(0, 2): [("oT", 0)], (0, 3): [("oT", 1), ("oT", 2)], (0, 5): [("oT", 3)],
          (0, 7): [("onT", 0), ("onT", 1)], (0, 9): [("stats1", 0)], (0, 11): [("wo", 0)],
          (0, 13): [("wo", 1)], (0, 16): [("stats2", 0)], (1, 0): [("rows2", 0)],
          (1, 3): [("h2T", 0)], (1, 4): [("h2T", 1)], (1, 5): [("rows1", 0)], (1, 7): [("h1T", 0)],
          (1, 8): [("h1T", 1)], (1, 10): [("logit", 0)], (1, 11): [("top", 0)],
          (1, 14): [("qk", 0), ("qk", 1)], (2, 1): [("e16", 0)], (2, 4): [("gates", 0), ("qk", 2)],
          (2, 5): [("gateT", 0)], (2, 7): [("qk", 3)], (2, 9): [("v", 0)], (2, 12): [("v", 1)],
          (2, 17): [("final", 0)], (3, 8): [("xg", 0)]}
EARLY = 2
WSPLIT = {(-1, 2, 10): 0, (-1, 2, 11): 1, (-1, 2, 12): 2, (0, 0, 3): 3, (0, 0, 7): 4, (0, 0, 11): 5,
          (0, 2, 11): 6, (0, 3, 9): 7}
for (_, _s, _u), _n in WSPLIT.items():
    EXTRAS[_s, _u] = EXTRAS.get((_s, _u), []) + [("wsplit", _n)]
SPLIT = (0, 2)
SPLIT_UNITS = [u for u in range(U) if (u // 2) % TT in SPLIT]
LO_VECTOR = (4, 5, 8, 9)
NPF = 2
NO_MAX = {0: (3, 5, 8), 1: (0, 11, 12), 2: (0, 10), 3: (0, 15)}


def slot_order(s):
    out = []
    maxima = [("max", (s + 1) * U + u) if s < 3 else ("max0", u) for u in range(U)]
    downs = [("down", d) for d in range(TT * SETS[DOWN_SET[s]], TT * SETS[DOWN_SET[s] + 1])]
    ups = [("up", c) for c in range(*SETS[UP_SET[s]:UP_SET[s] + 2])]
    for u in range(U):
        out += EXTRAS.get((s, u), [])
        if u not in NO_MAX[s]:
            out.append(maxima.pop(0))
        if u >= EARLY:
            out.append(("exp", s * U + u))
        if u - 1 in SPLIT_UNITS:
            out.append(("plo", s * U + u - 1))
        left = U - 1 - u
        while downs and len(downs) * (U - 1) > left * TT * SETLEN:
            out.append(downs.pop(0))
    assert not downs
    if U - 1 in SPLIT_UNITS:
        out.append(("plo", s * U + U - 1))
    for j, up in enumerate(ups):
        out += EXTRAS.get((s, U + j), [])
        if j == 3:
            out += maxima + [("maxT", s + 1) if s < 3 else ("maxT0", 0)]
            maxima = []
        out.append(up)
        if j < 2:
            out += maxima[:2]
            maxima = maxima[2:]
        if j >= 1:
            out.append(("gated", up[1] - 1))
        if j >= 3:
            out.append(("pv", s * TT + j - 3))
    out.append(("gated", ups[-1][1]))
    for kc in range(len(ups) - 3, TT):
        out.append(("pv", s * TT + kc))
        if kc >= TT - EARLY:
            out.append(("exp", (s + 1) * U + kc - TT + EARLY) if s < 3 else ("exp0", kc - TT + EARLY))
    return out


ORDER = [(s, item) for s in range(G) for item in slot_order(s)]
V_KINDS = ("max", "max0", "maxT", "maxT0", "oT", "wo", "v", "logit", "gateT")
R_KINDS = ("exp", "exp0", "onT", "h1T", "qk", "h2T", "up")
NV, NRB = 2, 3
PER = {"max": 64, "maxT": 4, "exp": 64, "oT": 4, "onT": 2, "wo": 2, "v": 2, "logit": 1, "gateT": 1,
       "h1T": 2, "qk": 4, "h2T": 2, "up": NEX, "pv": 16, "down": NEX * TT}


def true_item(item):
    kind, n = item
    if kind in ("max0", "maxT0", "exp0"):
        return kind[:-1], n, 1
    if kind in ("h1T", "qk", "v", "stats1", "rows1"):
        return kind, n, 1
    if kind == "up" or kind == "gated":
        return kind, n, -1 if SET_OF[n] < 2 else -2
    if kind == "down":
        return kind, n, -1 if SET_OF[n // TT] < 1 else -2
    if kind == "final":
        return kind, n, -2
    return kind, n, 0 if kind in ("max", "maxT", "exp", "pv", "plo", "xg") else -1


def ring(kinds, banks):
    seq = [item for _, item in ORDER if item[0] in kinds]
    seq += [None] * (-len(seq) % banks)
    found = {}
    for j, item in enumerate(seq):
        users = [(seq[(j - banks * r) % len(seq)], (j - banks * r) // len(seq)) for r in range(1, 60)]
        users = [user for user in users if user[0]]
        found[item] = (j % banks, users)
    return found


RINGS = {**ring(V_KINDS, NV), **ring(R_KINDS, NRB)}


def exists(b):
    return not isinstance(b, int) or 0 <= b < B


def lo_count(vector, n):
    return sum(m % U in SPLIT_UNITS and (m % U in LO_VECTOR) == vector for m in range(n))


def lo_place(n):
    units = [m for m in range(G * U) if m % U in SPLIT_UNITS]
    j = units.index(n)
    return j % NPF, units[(j - NPF) % len(units)], (j - NPF) // len(units)


assert G * len(SPLIT_UNITS) % NPF == 0 and all(2 * n in SPLIT or 2 * n + 1 in SPLIT for n in range(TT // 2))


def is_at(i, n):
    return isinstance(i, int) and i == n


def wait(eng, sem, per, b, k):
    value = b * per + k
    if isinstance(value, int) and value <= 0:
        return
    eng.wait_ge(sem, value)


def block_kernel(nc, x, c_t, wmod, wqkvo, bqk_in, bv, bo, w_up, w_down, router, out):
    q_d = nc.dram_tensor("q_parts", (2, DC, P, S), F16, kind="Internal").ap()
    k_d = nc.dram_tensor("k_parts", (2, DC, P, S), F16, kind="Internal").ap()
    gmod_d = nc.dram_tensor("gate_mods", (B, 2 * D), F32, kind="Internal").ap()
    tmod_d = nc.dram_tensor("feature_mods", (B, P, 8), F32, kind="Internal").ap()
    gate_d = nc.dram_tensor("gates_by_expert", (NR, S), F32, kind="Internal").ap()

    ctx = ExitStack()
    with ctx:
        def sb(name, shape, dt=F32):
            return ctx.enter_context(nc.sbuf_tensor(name, shape, dt))

        def sem(name):
            return ctx.enter_context(nc.semaphore(name))

        ident = sb("ident", [P, P])
        ident16 = sb("ident16", [P, P], F16)
        expert_no = sb("expert_no", [P, NR], I32)
        minus_half = sb("minus_half", [P, TT])
        w4 = [sb(f"wqkvo_{n}", [P, 4, DC, D], F16) for n in ("hi", "lo")]
        wr = [sb(f"router_{n}", [P, DC, NR], F16) for n in ("hi", "lo")]
        wu = [sb(f"up_{n}", [P, DC, NEX * E], F16) for n in ("hi", "lo")]
        wd = [sb(f"down_{n}", [P, NEX, D], F16) for n in ("hi", "lo")]
        bqk = sb("bqk", [P, 4])
        bv_all = sb("bv_all", [P, D])
        bo_all = sb("bo_all", [P, D])
        mod_pre = sb("mod_pre", [P, 8])
        mod_post = sb("mod_post", [P, 8])
        ga_all, gb_all = sb("ga_all", [P, 1, D]), sb("gb_all", [P, 1, D])
        x_pre = sb("x_pre", [P, TT, D])
        x_post2 = [sb(f"x_post{b}", [P, TT, D]) for b in range(2)]
        rows = sb("rows", [P, TT, D])
        f_ring = sb("f_ring", [P, 2, S])
        h1 = [sb(f"h1_{n}", [P, DC, S], F16) for n in ("hi", "lo")]
        qk = [sb(f"qk_{n}", [P, 2, S], F16) for n in ("hi", "lo")]
        z2 = [[sb(f"z{b}_{n}", [P, DC, S], F16) for n in ("hi", "lo")] for b in range(2)]
        q_aug = [sb(f"q_aug{n}", [P, H // 2, S], F16) for n in range(2)]
        k_aug = [sb(f"k_aug{n}", [P, H // 2, S], F16) for n in range(2)]
        v_aug = [sb(f"v_aug{b}", [P, TT, VROW]) for b in range(2)]
        neg_max = sb("neg_max", [P, TT, P], F16)
        probs = sb("probs", [P, U, S])
        prob_f = sb("prob_f", [P, NPF, S])
        o_raw = sb("o_raw", [P, G, S])
        act = [sb(f"act_{n}", [P, SETLEN, S], F16) for n in ("hi", "lo")]
        gelu = sb("gelu", [P, NGELU, S])
        gates = sb("gates", [P, 8, S])
        gate_rows = rows[0:NR, 0:2, :].rearrange("p t d -> p (t d)")
        v_full = rows[:, 2:4, :]
        stats = sb("stats", [P, TT, 6])
        mv = [sb(f"mean_var{n}", [P, TT, 2]) for n in range(2)]
        rstd = [sb(f"rstd{n}", [P, TT]) for n in range(2)]
        rsum = sb("rsum", [P, TT, H])
        logits = sb("logits", [P, TT, NR])
        top8 = sb("top8", [P, TT, 8])
        idx8 = sb("idx8", [P, TT, 8], U32)
        hit = sb("hit", [P, TT, TOPK, NR])
        ga_bo = hit[:].rearrange("p t k e -> p (t k e)")
        chosen = sb("chosen", [P, TT, NR])
        shifted = sb("shifted", [P, TT, NR])
        e16 = sb("e16", [P, TT, NR])
        esum = sb("esum", [P, TT])

        wmod_st = probs[:, 0:6, :].rearrange("p a n -> p (a n)").rearrange("p (c n) -> p c n", c=DC)
        w4_st = o_raw[:, :, :].rearrange("p (w c) (a n) -> p (w c a) n", w=4, n=D)
        w_st = gates[:, :, :].rearrange("p a n -> p (a n)")[:, 0:NST * WL].rearrange("p (k n) -> p k n", k=NST)
        silu = probs[:, 6, 0:DC * B].rearrange("p (c b) -> p c b", c=DC)
        silu_t = probs[:, 7, 0:DC * B].rearrange("p (c b) -> p c b", c=DC)
        ct_st = probs[:, 8, 0:DC * B].rearrange("p (c b) -> p c b", c=DC)
        wr_st = probs[:, 9, 0:DC * NR].rearrange("p (c n) -> p c n", c=DC)
        tmod_st = probs[:, 10, 0:8 * B].rearrange("p (b k) -> p b k", b=B)
        gm = [probs[0:B, 11 + n, 0:2 * D] for n in range(3)]

        VB = [ctx.enter_context(nc.psum_tensor(f"vector_bank{n}", [P, S], F32)) for n in range(NV)]
        RB = [ctx.enter_context(nc.psum_tensor(f"scalar_bank{n}", [P, S], F32)) for n in range(NRB)]
        OB = ctx.enter_context(nc.psum_tensor("pv_bank", [P, S], F32))
        DB = [ctx.enter_context(nc.psum_tensor(f"down_bank{n}", [P, S], F32)) for n in range(2)]

        def p_part(n, lo):
            return probs[:, n % U, :].bitcast(F16)[:, S * lo:S * (lo + 1)]

        def v_part(p, kc, lo):
            return v_aug[p][:, kc, :].bitcast(F16)[:, VROW * lo:VROW * (lo + 1)]

        def heads_of(row):
            return row[:, 0:H * VW].rearrange("p (h w) -> p h w", h=H)[:, :, 1:VW]

        def piece(parts, n):
            part = parts[n // (NW // 2)]
            flat = part[:].rearrange("p a n -> p (a n)")
            n = n % (NW // 2)
            return flat[:, WL * n:WL * (n + 1)]

        made = {k: sem(f"made_{k}") for k in PER}
        taken = {k: sem(f"taken_{k}") for k in PER}
        s_const = sem("constants_ready")
        s_passed = sem("waits_passed")
        s_w4, s_mod_in = [sem("wqk_loaded"), sem("wvo_loaded")], [sem("mod0_loaded"), sem("mod1_loaded")]
        s_small, s_w4hi = sem("biases_loaded"), sem("w4_hi")
        s_w4s, s_silu, s_setup_mm, s_setup_v = sem("w4_split"), sem("silu_steps"), sem("mods_made"), sem("setup_vector")
        s_gm_st = sem("mods_stored")
        s_wst = [sem(f"expert_weights_staged{n}") for n in range(NST)]
        s_whi, s_wlo = sem("expert_weights_hi"), sem("expert_weights_lo")
        s_ct, s_mod0 = sem("c_loaded"), sem("first_mods_made")
        s_xpre, s_mpre = sem("x_pre_loaded"), sem("mod_pre_loaded")
        s_xpost, s_mpost = sem("x_post_loaded"), sem("mod_post_loaded")
        s_ga, s_gb = sem("ga_loaded"), sem("gb_loaded")
        s_ln1, s_ln2 = sem("ln1_steps"), sem("ln2_steps")
        s_rs1, s_rs2 = sem("rstd1_steps"), sem("rstd2_steps")
        s_onlo, s_h1lo, s_qklo, s_h2lo = sem("attention_lo"), sem("h1_lo"), sem("qk_lo"), sem("h2_lo")
        s_qkst, s_aug = [sem("qk0_stored"), sem("qk1_stored")], sem("score_operands_loaded")
        s_xg = sem("residual_plus_gated_bias")
        s_on = sem("normalised_steps")
        s_x2 = sem("attention_added")
        s_plo = {False: sem("probs_lo_by_gpsimd"), True: sem("probs_lo_by_vector")}
        s_v, s_vlo = sem("v_steps"), sem("v_lo")
        s_top, s_e16 = sem("router_steps"), sem("router_exp")
        s_gst, s_gld = sem("gates_stored"), [sem("gates0_loaded"), sem("gates1_loaded")]
        s_ehi, s_gated, s_elo = sem("expert_hi_made"), sem("expert_gated"), sem("expert_lo_made")
        s_fin, s_sum, s_out = sem("experts_times_gb"), sem("experts_added"), sem("out_stored")
        s_aug0, s_aug1 = sem("first_score_operand_constants"), sem("other_operand_constants")

        def wait_apart(eng, sem, per, b, k):
            wait(eng, sem, per, b, k)
            if not isinstance(b, int):
                eng.sem_inc(s_passed, 1)

        block = ctx.enter_context(nc.Block())

        def bank(item):
            kind = item[0]
            n = RINGS[item][0]
            return (VB if kind in V_KINDS else RB)[n]

        def wait_bank(eng, item, i):
            for prev, back in RINGS[item][1]:
                kind, n, lag = true_item(prev)
                b = i + back + lag
                if exists(b) or (not isinstance(i, int)):
                    wait(eng, taken[kind], PER[kind], b, n + 1)
                    return

        def iterations(eng, body):
            for i in (-1, 0, 1, 2):
                body(i, i % 2)
            with eng.Fori(0, 2) as j:
                body(j * 2 + 3, 1)
                body(j * 2 + 4, 0)
            for i in (7, 8, 9):
                body(i, i % 2)

        def items(i, s):
            for item in slot_order(s):
                kind, n, lag = true_item(item)
                if kind == "wsplit":
                    at = [a for a, piece in WSPLIT.items() if piece == n][0]
                    if is_at(i, at[0]):
                        yield item, kind, n, i
                elif exists(i + lag):
                    yield item, kind, n, i + lag


        @block.sync
        def _(sp):
            def stage(n):
                if n >= NST:
                    sp.wait_ge(s_wlo, n - NST + 1)
                src = w_up[P * (n // 2):P * (n // 2 + 1), WL * (n % 2):WL * (n % 2 + 1)] if n < NW // 2 else \
                    w_down[:, WL * (n - NW // 2):WL * (n - NW // 2 + 1)]
                sp.dma_start(w_st[:, n % NST, :], src).then_inc(s_wst[n % NST], 16)

            sp.dma_start(ct_st, c_t.rearrange("(c p) b -> p c b", c=DC)).then_inc(s_ct, 16)
            sp.dma_start(x_pre[:], x[0].rearrange("(t p) d -> p t d", t=TT)).then_inc(s_xpre, 16)
            mods = wmod.rearrange("(c p) n -> p c n", c=DC)
            sp.dma_start(wmod_st[:, :, 0:2 * D], mods[:, :, 0:2 * D]).then_inc(s_mod_in[0], 16)
            for m in range(2):
                sp.dma_start(w4_st[:, 4 * m:4 * m + 4, :],
                             wqkvo[2 * m:2 * m + 2].rearrange("w (c p) n -> p (w c) n", c=DC)).then_inc(s_w4[m], 16)
            sp.dma_start(bqk[:], bqk_in).then_inc(s_small, 16)
            sp.dma_start(bv_all[:], bv.partition_broadcast(P)).then_inc(s_small, 16)
            sp.dma_start(bo_all[:], bo.partition_broadcast(P)).then_inc(s_small, 16)
            sp.dma_start(wr_st, router.rearrange("(c p) n -> p c n", c=DC)).then_inc(s_small, 16)
            sp.dma_start(wmod_st[:, :, 2 * D:6 * D], mods[:, :, 2 * D:6 * D]).then_inc(s_mod_in[1], 16)
            for n in range(NST):
                stage(n)
            sp.wait_ge(s_aug0, 2)
            sp.wait_ge(s_aug1, 2 + 2 * TT)

            def body(i, par):
                b = i + 1
                if is_at(i, 0):
                    sp.wait_ge(s_gm_st, 32)
                if exists(b) and not is_at(i, -1):
                    wait_apart(sp, s_ln1, 12, b, 0)
                    sp.dma_start(x_pre[:], x[b].rearrange("(t p) d -> p t d", t=TT)).then_inc(s_xpre, 16)
                    wait_apart(sp, taken["h1T"], 2, b, 0)
                    sp.dma_start(mod_pre[:], tmod_d[b]).then_inc(s_mpre, 16)
                if is_at(i, 0):
                    for n in (6, 7):
                        stage(n)
                b = i + 1
                if exists(b):
                    qa, ka = q_aug[1 - par], k_aug[1 - par]

                    def store(n):
                        wait_apart(sp, s_qklo, 4, b, n + 1)
                        for part in range(2):
                            sp.dma_start((q_d, k_d)[n // 2][part, n % 2], qk[part][:, n % 2, :]).then_inc(s_qkst[n % 2], 16)

                    def load(n, odd):
                        for row, part in ((0, 0), (16, n == 0), (48, n)):
                            src = (q_d, k_d)[n][int(part)].rearrange("c (p two d) t -> two d (c p) t", two=2, d=DH)[odd]
                            at = 64 * odd + row
                            sp.dma_start((qa, ka)[n][at:at + DH, :, :], src).then_inc(s_aug, 16)

                    wait_apart(sp, s_aug, 16 * 14, b, 0)
                    store(0)
                    store(1)
                    for m in range(2):
                        wait_apart(sp, s_qkst[m], 64, b, 32)
                    wait_apart(sp, made["exp"], 64, i, 0)
                    wait_apart(sp, made["max"], 64, i, 0)
                    load(0, 0)
                    store(2)
                    load(0, 1)
                    store(3)
                    for odd in range(2):
                        at = 64 * odd + 32
                        sp.dma_start(qa[at:at + 1, :, :], qa[at + 1:at + 2, :, :]).then_inc(s_aug, 16)
                    for m in range(2):
                        wait_apart(sp, s_qkst[m], 64, b, 64)
                    load(1, 0)
                    load(1, 1)
                b = i - 1
                if is_at(i, -1):
                    sp.wait_ge(s_setup_v, 8)
                    sp.dma_start(tmod_d.rearrange("b p k -> p b k"), tmod_st).then_inc(s_gm_st, 16)
                    sp.dma_start(gmod_d, gm[2]).then_inc(s_gm_st, 16)
                    for n in (3, 4, 5):
                        stage(n)
                if exists(b):
                    wait_apart(sp, taken["gateT"], 1, b, 1)
                    for m in range(2):
                        wait_apart(sp, s_gld[m], 32, b, 0)
                    sp.dma_start(gate_d, gate_rows).then_inc(s_gst, 16)
                    wait_apart(sp, s_gst, 16, b, 16)
                for quarter in range(4):
                    if quarter == 2 and exists(i - 2):
                        wait_apart(sp, s_sum, 2, i - 2, 2)
                        sp.dma_start(out[i - 2].rearrange("(t p) d -> p t d", t=TT), x_post2[par][:]).then_inc(s_out, 16)
                    if quarter == 2 and exists(b):
                        wait_apart(sp, s_fin, 2, b, 0)
                        sp.dma_start(gb_all[:, 0, :], gmod_d[b, D:2 * D].partition_broadcast(P)).then_inc(s_gb, 16)
                    if quarter == 2 and exists(i):
                        wait_apart(sp, taken["wo"], 2, i, 0)
                        sp.dma_start(ga_all[:, 0, :], gmod_d[i, 0:D].partition_broadcast(P)).then_inc(s_ga, 16)
                        wait_apart(sp, taken["h2T"], 2, i, 0)
                        sp.dma_start(mod_post[:], tmod_d[i]).then_inc(s_mpost, 16)
                        wait_apart(sp, s_out, 16, i - 1, 0)
                        sp.dma_start(x_post2[par][:], x[i].rearrange("(t p) d -> p t d", t=TT)).then_inc(s_xpost, 16)
                    if exists(b):
                        wait_apart(sp, s_elo, NEX, b, NSH + 4 * quarter + 4 - 8 - (NSH if quarter < 2 else 0))
                        at = 4 * (quarter % 2)
                        sp.dma_start(gates[:, at:at + 4, :], gate_d[4 * quarter:4 * quarter + 4, :].partition_broadcast(P)
                                     ).then_inc(s_gld[quarter % 2], 16)

            iterations(sp, body)
            sp.wait_ge(s_out, 16 * B)
            sp.wait_ge(s_gst, 16 * B)
            for m in range(2):
                sp.wait_ge(s_qkst[m], 64 * B)

        @block.gpsimd
        def _(pool):
            pool.memset(minus_half[:], -0.5).then_inc(s_const, 1)
            pool.memset(ident[:], 0.0).then_inc(s_const, 1)
            pool.memset(ident16[:], 0.0).then_inc(s_const, 1)
            pool.iota(expert_no[:], [[1, NR]], base=0, channel_multiplier=0).then_inc(s_const, 1)
            pool.wait_ge(s_const, 4)
            for m in (ident, ident16):
                pool.affine_select(out=m[:], in_=m[:], compare_op=ALU.not_equal, fill=1.0, base=0,
                                   pattern=[[-1, P]], channel_multiplier=1).then_inc(s_const, 1)
            pool.memset(neg_max[:], 0.0).then_inc(s_const, 1)
            pool.memset(q_aug[0][:].bitcast(U32), 0).then_inc(s_aug0, 1)
            pool.memset(k_aug[0][:].bitcast(U32), 0x3C003C00).then_inc(s_aug0, 1)

            def power(b, m, r, s_stats, s_rs):
                wait_apart(pool, s_stats, 12, b, 8)
                pool.tensor_scalar(r[:], m[:, :, 1], EPS, None, ALU.add).then_inc(s_rs, 1)
                wait(pool, s_rs, 2, b, 1)
                pool.tensor_tensor(r[:], r[:], minus_half[:], ALU.pow).then_inc(s_rs, 1)

            power(0, mv[0], rstd[0], s_ln1, s_rs1)
            def lo_part(kind, n, b, hi, lo, s_lo):
                wait(pool, taken[kind], PER[kind], b, n + 1)
                pool.tensor_tensor(lo, f_ring[:, n % 2, :], hi, ALU.subtract).then_inc(s_lo, 1)

            def body(i, par):
                z = z2[1 - par]
                for s in range(G):
                    for item, kind, n, b in items(i, s):
                        if kind == "wsplit":
                            pool.wait_ge(s_whi, n + 1)
                            pool.tensor_tensor(piece((wu[1], wd[1]), n), w_st[:, n % NST, :], piece((wu[0], wd[0]), n),
                                               ALU.subtract).then_inc(s_wlo, 1)
                        elif kind == "xg":
                            x_post = x_post2[par]
                            wait(pool, s_ga, 16, b, 16)
                            wait(pool, s_top, 15, b, 0)
                            pool.tensor_tensor(ga_bo, ga_all[:, 0, :], bo_all[:], ALU.mult).then_inc(s_xg, 1)
                            wait(pool, s_xg, 2, b, 1)
                            wait(pool, s_xpost, 16, b, 16)
                            pool.tensor_tensor(x_post[:], x_post[:], ga_bo.unsqueeze(1).broadcast_to([P, TT, D]), ALU.add).then_inc(s_xg, 1)
                        elif kind == "plo" and n % U not in LO_VECTOR:
                            wait(pool, taken["exp"], 64, b, n + 1)
                            pool.tensor_tensor(p_part(n, 1), prob_f[:, lo_place(n)[0], :], p_part(n, 0),
                                               ALU.subtract).then_inc(s_plo[False], 1)
                        elif kind == "v":
                            wait(pool, s_v, 2, b, n + 1)
                            for t in range(2):
                                if 2 * n + t in SPLIT:
                                    lo, hi = (heads_of(v_part(1 - par, 2 * n + t, k)) for k in (1, 0))
                                    ins = pool.tensor_tensor(lo, v_full[:, t, :].rearrange("p (h w) -> p h w", h=H), hi,
                                                             ALU.subtract)
                            ins.then_inc(s_vlo, 1)
                        elif kind == "stats1" and not is_at(i, -1):
                            power(b, mv[0], rstd[0], s_ln1, s_rs1)
                        elif kind == "stats2":
                            power(b, mv[1], rstd[1], s_ln2, s_rs2)
                        if kind == "h1T":
                            if n == 0:
                                wait(pool, made["v"], 2, b, 0)
                            lo_part(kind, n, b, h1[0][:, n, :], h1[1][:, n, :], s_h1lo)
                        elif kind == "qk":
                            lo_part(kind, n, b, qk[0][:, n % 2, :], qk[1][:, n % 2, :], s_qklo)
                        elif kind == "h2T":
                            lo_part(kind, n, b, z[0][:, n, :], z[1][:, n, :], s_h2lo)
                        elif kind == "onT":
                            lo_part(kind, n, b, z[0][:, n, :], z[1][:, n, :], s_onlo)
                        elif kind == "wo":
                            wait(pool, taken["wo"], 2, b, n + 1)
                            wait_apart(pool, s_xg, 2, b, 2)
                            xs = x_post2[1 - par][:, 2 * n:2 * n + 2, :]
                            pool.tensor_tensor(xs, xs, rows[:, 2 * n:2 * n + 2, :], ALU.add).then_inc(s_x2, 1)
                        elif kind == "final":
                            for m in range(2):
                                wait(pool, s_fin, 2, b, m + 1)
                                xs = x_post2[par][:, 2 * m:2 * m + 2, :]
                                pool.tensor_tensor(xs, xs, rows[:, 2 * m:2 * m + 2, :], ALU.add).then_inc(s_sum, 1)
                        elif kind == "gated":
                            c = n - SETS[SET_OF[n]]
                            wait(pool, s_ehi, NEX, b, n + 1)
                            pool.tensor_tensor(act[1][:, c, :], gelu[:, n % NGELU, :], act[0][:, c, :],
                                               ALU.subtract).then_inc(s_elo, 1)
            iterations(pool, body)

        @block.scalar
        def _(scalar):
            scalar.wait_ge(s_ct, 16)
            scalar.activation(silu_t, ct_st, ACT.Exp, scale=-1.0).then_inc(s_silu, 1)
            for m in range(2):
                scalar.wait_ge(s_w4[m], 16)
                scalar.activation(w4[0][:, 2 * m:2 * m + 2].rearrange("p w c n -> p (w c n)"),
                                  w4_st[:, 4 * m:4 * m + 4, :].rearrange("p a n -> p (a n)"), ACT.Copy).then_inc(s_w4hi, 1)
            scalar.wait_ge(s_small, 64)

            def split_out(kind, n, b, src, hi, f, scale, bias):
                scalar.activation(hi, src, ACT.Identity, bias=bias, scale=scale)
                scalar.activation(f, src, ACT.Identity, bias=bias, scale=scale).then_inc(taken[kind], 1)

            def body(i, par):
                for s in range(G):
                    for item, kind, n, b in items(i, s):
                        if kind == "e16":
                            wait(scalar, s_top, 15, b, 9)
                            scalar.activation(e16[:], shifted[:], ACT.Exp).then_inc(s_e16, 1)
                        if kind == "wsplit":
                            scalar.wait_ge(s_wst[n % NST], 16 * (n // NST + 1))
                            scalar.activation(piece((wu[0], wd[0]), n), w_st[:, n % NST, :], ACT.Copy).then_inc(s_whi, 1)
                        if item[0] not in R_KINDS:
                            continue
                        src = bank(item)
                        wait(scalar, made[kind], PER[kind], b, n + 1)
                        if kind == "exp":
                            g, kc = n // U, (n % U // 2) % TT
                            if n % 2 == 0:
                                wait(scalar, made["pv"], G * TT, b, (g - 1) * TT + kc + 1)
                            if n % U in SPLIT_UNITS:
                                scalar.activation(p_part(n, 0), src[:], ACT.Exp, scale=SCALE)
                                place, before, back = lo_place(n)
                                by_vector = before % U in LO_VECTOR
                                wait(scalar, s_plo[by_vector], lo_count(by_vector, G * U), b + back,
                                     lo_count(by_vector, before + 1))
                                scalar.activation(prob_f[:, place, :], src[:], ACT.Exp, scale=SCALE).then_inc(taken[kind], 1)
                            else:
                                scalar.activation(probs[:, n % U, :], src[:], ACT.Exp, scale=SCALE).then_inc(taken[kind], 1)
                        elif kind == "h1T":
                            if n == 0:
                                if is_at(i, -1):
                                    scalar.wait_ge(s_mod0, 2)
                                wait(scalar, s_mpre, 16, b, 0)
                                wait(scalar, made["v"], 2, b, 0)
                            if exists(i - 1):
                                wait(scalar, s_h2lo, 2, i - 1, n + 1)
                            else:
                                wait(scalar, s_qklo, 4, b, 0)
                            split_out(kind, n, b, src[:], h1[0][:, n, :], f_ring[:, n, :],
                                      mod_pre[:, 2 + n:3 + n], mod_pre[:, n:n + 1])
                        elif kind == "qk":
                            if n < 2:
                                wait(scalar, s_h1lo, 2, b, 2)
                                wait(scalar, s_qkst[n], 64, b, 0)
                            else:
                                wait(scalar, s_qklo, 4, b, n - 1)
                                wait(scalar, s_qkst[n - 2], 64, b, 32)
                            scalar.activation(qk[0][:, n % 2, :], src[:], ACT.Identity, bias=bqk[:, n:n + 1])
                            scalar.activation(f_ring[:, n % 2, :], src[:], ACT.Identity, bias=bqk[:, n:n + 1]).then_inc(taken[kind], 1)
                        elif kind == "onT":
                            z = z2[1 - par]
                            wait(scalar, s_qklo, 4, min(i, B - 1) if isinstance(i, int) else i, 4)
                            wait(scalar, made["up"], NEX, b - 1, 0)
                            wait(scalar, made["logit"], 1, b - 1, 0)
                            scalar.activation(z[0][:, n, :], src[:], ACT.Copy)
                            scalar.activation(f_ring[:, n, :], src[:], ACT.Copy).then_inc(taken[kind], 1)
                        elif kind == "h2T":
                            if n == 0:
                                wait(scalar, s_mpost, 16, b, 16)
                            z = z2[1 - par]
                            wait(scalar, s_onlo, 2, b, n + 1)
                            wait(scalar, made["wo"], 2, b, 2)
                            split_out(kind, n, b, src[:], z[0][:, n, :], f_ring[:, n, :],
                                      mod_post[:, 6 + n:7 + n], mod_post[:, 4 + n:5 + n])
                        elif kind == "up":
                            wait(scalar, s_elo, NEX, b, n - NGELU + 1)
                            scalar.activation(gelu[:, n % NGELU, :], src[:], ACT.Gelu).then_inc(taken[kind], 1)

            iterations(scalar, body)

        @block.vector
        def _(dve):
            def ln_stats(src, m, s_ln, b, ready, per, k):
                for t in range(TT):
                    if t == 0:
                        wait(dve, ready, per, b, k)
                    dve.bn_stats(stats[:, t, :], src[:, t, :]).then_inc(s_ln, 1)
                for t in range(TT):
                    if t == 0:
                        wait_apart(dve, s_ln, 12, b, 4)
                    dve.bn_aggr(m[:, t, :], stats[:, t, :]).then_inc(s_ln, 1)

            def ln_rows(src, m, r, s_ln, s_rs, b):
                wait(dve, s_rs, 2, b, 2)
                for t in range(TT):
                    dve.tensor_scalar(rows[:, t, :], src[:, t, :], m[:, t, 0:1], r[:, t:t + 1],
                                      ALU.subtract, ALU.mult).then_inc(s_ln, 1)

            dve.wait_ge(s_silu, 1)
            dve.tensor_scalar(silu_t, silu_t, 1.0, None, ALU.add).then_inc(s_silu, 1)
            dve.wait_ge(s_silu, 2)
            dve.reciprocal(silu_t, silu_t).then_inc(s_silu, 1)
            dve.wait_ge(s_silu, 3)
            dve.tensor_tensor(silu, silu_t, ct_st, ALU.mult).then_inc(s_silu, 1)
            ln_stats(x_pre, mv[0], s_ln1, 0, s_xpre, 16, 16)
            ln_rows(x_pre, mv[0], rstd[0], s_ln1, s_rs1, 0)
            src, src2 = (m[:, 0:8 * B].rearrange("p (k b) -> p b k", k=8) for m in (DB[0], OB))
            dve.wait_ge(s_setup_mm, 1)
            for n, add in ((0, 0.0), (2, 1.0)):
                dve.tensor_scalar(mod_pre[:, n:n + 2], src[:, 0, n:n + 2], add, None, ALU.add).then_inc(s_mod0, 1)
            for m in range(2):
                lo4, hi4 = (w4[k][:, 2 * m:2 * m + 2].rearrange("p w c n -> p (w c n)") for k in (1, 0))
                dve.wait_ge(s_w4hi, m + 1)
                dve.tensor_tensor(lo4, w4_st[:, 4 * m:4 * m + 4, :].rearrange("p a n -> p (a n)"), hi4,
                                  ALU.subtract).then_inc(s_w4s, 1)
            dve.memset(q_aug[1][:].bitcast(U32), 0).then_inc(s_aug1, 1)
            dve.memset(k_aug[1][:].bitcast(U32), 0x3C003C00).then_inc(s_aug1, 1)
            for n in range(2):
                for kc in range(TT):
                    if kc in SPLIT:
                        dve.memset(v_part(n, kc, 0), 1.0)
                        dve.memset(v_part(n, kc, 1), 0.0).then_inc(s_aug1, 1)
                    else:
                        dve.memset(v_aug[n][:, kc, :], 1.0).then_inc(s_aug1, 1)
            dve.wait_ge(s_setup_mm, 2)
            for n, add in ((0, 0.0), (2, 1.0), (4, 0.0), (6, 1.0)):
                dve.tensor_scalar(tmod_st[:, :, n:n + 2], (src if n < 4 else src2)[:, :, n:n + 2], add, None, ALU.add).then_inc(s_setup_v, 1)
            g = DB[1][0:B, 0:2 * D]
            dve.wait_ge(s_setup_mm, 3)
            dve.tensor_scalar(gm[0], g, 0.0, 2.0, ALU.is_ge, ALU.mult).then_inc(s_setup_v, 1)
            dve.tensor_scalar(gm[1], g, -1.0, MINGATE, ALU.mult, ALU.max).then_inc(s_setup_v, 1)
            dve.wait_ge(s_setup_v, 6)
            dve.tensor_tensor(gm[1], gm[1], g, ALU.max).then_inc(s_setup_v, 1)
            dve.wait_ge(s_setup_v, 7)
            dve.scalar_tensor_tensor(gm[2], gm[0], -1.0, gm[1], ALU.add, ALU.mult).then_inc(s_setup_v, 1)
            dve.wait_ge(s_small, 64)
            dve.tensor_copy(wr[0][:], wr_st).then_inc(s_setup_v, 1)
            dve.wait_ge(s_setup_v, 9)
            dve.tensor_tensor(wr[1][:], wr_st, wr[0][:], ALU.subtract).then_inc(s_setup_v, 1)

            def top_four(b):
                w = lambda k: wait_apart(dve, s_top, 15, b, k)
                wait_apart(dve, taken["logit"], 1, b, 1)
                for t in range(TT):
                    dve.max(top8[:, t, :], logits[:, t, :]).then_inc(s_top, 1)
                w(4)
                for t in range(TT):
                    dve.max_index(idx8[:, t, :], top8[:, t, :], logits[:, t, :]).then_inc(s_top, 1)
                dve.tensor_tensor(shifted[:], logits[:], top8[:, :, 0:1].broadcast_to([P, TT, NR]),
                                  ALU.subtract).then_inc(s_top, 1)
                w(8)
                dve.tensor_tensor(hit[:], idx8[:, :, 0:TOPK].unsqueeze(3).broadcast_to([P, TT, TOPK, NR]),
                                  expert_no[:].unsqueeze(1).unsqueeze(1).broadcast_to([P, TT, TOPK, NR]),
                                  ALU.is_equal).then_inc(s_top, 1)
                w(10)
                dve.tensor_reduce(chosen[:], hit[:].rearrange("p t k e -> p t e k"), AX.X, ALU.add).then_inc(s_top, 1)

            def gate_values(b):
                w = lambda k: wait_apart(dve, s_top, 15, b, k)
                wait(dve, s_e16, 1, b, 1)
                dve.tensor_reduce(esum[:], e16[:], AX.X, ALU.add).then_inc(s_top, 1)
                w(12)
                dve.reciprocal(esum[:], esum[:]).then_inc(s_top, 1)
                w(11)
                dve.tensor_tensor(chosen[:], chosen[:], e16[:], ALU.mult).then_inc(s_top, 1)
                w(14)
                dve.tensor_tensor(chosen[:], chosen[:], esum[:].unsqueeze(2).broadcast_to([P, TT, NR]),
                                  ALU.mult).then_inc(s_top, 1)

            def body(i, par):
                nb, pb = i + 1, i - 1
                x_post, z = x_post2[1 - par], z2[1 - par]
                for s in range(G):
                    for item, kind, n, b in items(i, s):
                        if kind == "stats1" and not is_at(i, -1):
                            if exists(pb):
                                wait(dve, s_ln2, 12, pb - 1, 8)
                            ln_stats(x_pre, mv[0], s_ln1, nb, s_xpre, 16, 16)
                        if kind == "rows1" and not is_at(i, -1):
                            if exists(pb):
                                wait(dve, made["h2T"], 2, pb, 2)
                            ln_rows(x_pre, mv[0], rstd[0], s_ln1, s_rs1, nb)
                        if kind == "top":
                            top_four(b)
                        if kind == "gates":
                            gate_values(b)
                        if kind == "final":
                            wait(dve, s_gb, 16, b, 16)
                            wait(dve, made["down"], NEX * TT, b, NEX * TT)
                            wait(dve, s_gst, 16, min(b + 1, B - 1) if isinstance(b, int) else b + 1, 16)
                            wait(dve, s_vlo, 2, min(b + 3, B - 1) if isinstance(b, int) else b + 3, 2)
                            for m in range(2):
                                dve.tensor_tensor(rows[:, 2 * m:2 * m + 2, :], DB[m][:].rearrange("p (t d) -> p t d", t=2),
                                                  gb_all[:, 0:1, :].broadcast_to([P, 2, D]), ALU.mult).then_inc(s_fin, 1)
                        if kind == "stats2":
                            wait(dve, s_ln1, 12, min(nb, B - 1) if isinstance(nb, int) else nb, 8)
                            ln_stats(x_post, mv[1], s_ln2, b, s_x2, 2, 2)
                        if kind == "rows2":
                            ln_rows(x_post, mv[1], rstd[1], s_ln2, s_rs2, pb)
                        if kind == "gated":
                            g = gelu[:, n % NGELU, :]
                            wait(dve, taken["up"], NEX, b, n + 1)
                            c = n - SETS[SET_OF[n]]
                            if c == 0:
                                wait(dve, made["down"], NEX * TT, b, n * TT)
                            if n < NSH:
                                dve.tensor_copy(act[0][:, c, :], g).then_inc(s_ehi, 1)
                            else:
                                quarter, rest = divmod(n - NSH, 4)
                                if rest == 0:
                                    wait(dve, s_gld[quarter % 2], 32, b, 16 * (quarter // 2 + 1))
                                dve.tensor_tensor(g, g, gates[:, (n - NSH) % 8, :], ALU.mult).then_inc(s_gated, 1)
                                wait(dve, s_gated, NR, b, n - NSH + 1)
                                dve.tensor_copy(act[0][:, c, :], g).then_inc(s_ehi, 1)
                        if kind == "plo" and n % U in LO_VECTOR:
                            wait(dve, taken["exp"], 64, b, n + 1)
                            dve.tensor_tensor(p_part(n, 1), prob_f[:, lo_place(n)[0], :], p_part(n, 0),
                                              ALU.subtract).then_inc(s_plo[True], 1)
                        if item[0] not in V_KINDS:
                            continue
                        src = bank(item)
                        wait(dve, made[kind], PER[kind], b, n + 1)
                        done = taken[kind]
                        if kind == "max":
                            u = n % U
                            at = 32 * (u // 8 * 2 + u % 2)
                            dve.tensor_reduce(neg_max[:, (u // 2) % TT, at:at + 1],
                                              src[:], AX.X, ALU.max, negate=True).then_inc(done, 1)
                        elif kind == "maxT":
                            qa = q_aug[par if b is i or n else 1 - par]
                            if item[0] == "maxT0":
                                qa = q_aug[1 - par]
                            for j in range(GH):
                                at = 32 + 64 * (j % 2)
                                ins = dve.tensor_copy(qa[at:at + 1, 2 * n + j // 2, :], src[:].bitcast(F16)[32 * j:32 * j + 1, 0:S])
                            ins.then_inc(done, 1)
                        elif kind == "oT":
                            o = src[:].rearrange("p (h w) -> p h w", h=H)
                            if n == 0 and exists(i):
                                wait(dve, made["h1T"], 2, i, 2)
                            if n == 0:
                                wait(dve, s_sum, 2, b - 1, 0)
                            dve.reciprocal(rsum[:, n, :], o[:, :, 0]).then_inc(s_on, 1)
                            wait(dve, s_on, 4, b, n + 1)
                            dve.tensor_tensor(rows[:, n, :].rearrange("p (h w) -> p h w", h=H), o[:, :, 1:VW],
                                              rsum[:, n, :].unsqueeze(2).broadcast_to([P, H, DH]), ALU.mult).then_inc(done, 1)
                        elif kind == "wo":
                            if n == 0:
                                wait(dve, s_ga, 16, b, 16)
                            dve.tensor_tensor(rows[:, 2 * n:2 * n + 2, :], src[:].rearrange("p (t d) -> p t d", t=2),
                                              ga_all[:, 0:1, :].broadcast_to([P, 2, D]), ALU.mult).then_inc(done, 1)
                        elif kind == "v":
                            if n == 0:
                                dve.wait_ge(s_aug1, 2 + 2 * TT)
                                wait(dve, made["pv"], G * TT, i, 0)
                            wait(dve, s_vlo, 2, b, n)
                            by_head = bv_all[:].rearrange("p (h w) -> p h w", h=H)
                            full = [v_full[:, t, :].rearrange("p (h w) -> p h w", h=H) for t in range(2)]
                            for t in range(2):
                                to = full[t] if 2 * n + t in SPLIT else heads_of(v_aug[1 - par][:, 2 * n + t, :])
                                ins = dve.tensor_tensor(to, src[:, t * D:(t + 1) * D].rearrange("p (h w) -> p h w", h=H),
                                                        by_head, ALU.add)
                            ins.then_inc(done, 1)
                            wait(dve, done, 2, b, n + 1)
                            for t in range(2):
                                if 2 * n + t in SPLIT:
                                    ins = dve.tensor_copy(heads_of(v_part(1 - par, 2 * n + t, 0)), full[t])
                            ins.then_inc(s_v, 1)
                        elif kind == "logit":
                            dve.tensor_copy(logits[:].rearrange("p t e -> p (t e)"), src[:, 0:TT * NR]).then_inc(done, 1)
                        elif kind == "gateT":
                            wait(dve, s_gst, 16, b, 0)
                            dve.tensor_copy(gate_rows, src[0:NR, :]).then_inc(done, 1)
                    if exists(i):
                        wait(dve, made["pv"], G * TT, i, TT * (s + 1))
                        wait(dve, made["oT"], 4, i, 0)
                        dve.tensor_copy(o_raw[:, s, :], OB[:]).then_inc(taken["pv"], 1)

            iterations(dve, body)

        @block.tensor
        def _(pe):
            def split_product(dst, pairs):
                terms = [(a, b) for st, mo in pairs for a, b in ((st[0], mo[0]), (st[0], mo[1]), (st[1], mo[0]))]
                for n, (a, b) in enumerate(terms):
                    ins = pe.matmul(dst, a, b, start=n == 0, stop=n == len(terms) - 1)
                return ins

            def modulations(part):
                pe.wait_ge(s_mod_in[min(part, 1)], 16)
                if part < 2:
                    for k, col in list(enumerate((0, D, 3 * D, 4 * D)))[2 * part:2 * part + 2]:
                        for half in range(2):
                            for c in range(DC):
                                o = (DB[0] if k < 2 else OB)[:, (2 * k + half) * B:(2 * k + half + 1) * B]
                                ins = pe.matmul(o, wmod_st[:, c, col + P * half:col + P * half + P], silu[:, c, :],
                                                start=c == 0, stop=c == DC - 1)
                else:
                    for k, col in enumerate((2 * D, 5 * D)):
                        for c in range(DC):
                            ins = pe.matmul(DB[1][0:B, D * k:D * k + D], silu[:, c, :], wmod_st[:, c, col:col + D],
                                            start=c == 0, stop=c == DC - 1)
                ins.then_inc(s_setup_mm, 1)

            pe.wait_ge(s_silu, 4)
            modulations(0)
            pe.wait_ge(s_const, 7)

            def unit(n):
                u = n % U
                return (n // U) * 2 + u // 8, 64 * (u % 2), (u // 2) % TT

            def body(i, par):
                for s in range(G):
                    for item, kind, n, b in items(i, s):
                        z = z2[par if kind == "up" and SET_OF[n] >= 2 else 1 - par]
                        if kind in V_KINDS or kind in R_KINDS:
                            wait_bank(pe, item, i)
                            dst = bank(item)
                        elif kind not in PER:
                            continue
                        sig = made[kind]
                        if kind in ("max", "exp"):
                            ahead = item[0] in ("max0", "exp0")
                            qa, ka = q_aug[1 - par if ahead else par], k_aug[1 - par if ahead else par]
                            pair, at, t = unit(n)
                            if item == ("max0", 0):
                                wait(pe, s_aug, 16 * 14, b, 16 * 14)
                            if kind == "exp" and n % U == 0:
                                wait(pe, taken["maxT"], 4, b, n // U + 1)
                            st, mo = (qa, ka) if kind == "max" else (ka, qa)
                            pe.matmul(dst[:], st[at:at + 64, pair, t * P:(t + 1) * P], mo[at:at + 64, pair, :],
                                      start=True, stop=True).then_inc(sig, 1)
                        elif kind == "maxT":
                            wait(pe, taken["max"], PER["max"], b, U * (n + 1))
                            d16 = dst[:].bitcast(F16)
                            for t in range(TT):
                                ins = pe.transpose(d16[:, t * P:(t + 1) * P], neg_max[:, t, :], ident16[:])
                            ins.then_inc(sig, 1)
                        elif kind == "pv":
                            g, kc = divmod(n, TT)
                            if kc == 0:
                                if g == 0:
                                    wait(pe, s_vlo, 2, b, 2)
                                wait(pe, taken["pv"], 4, b, g)
                            if kc == 0:
                                wait(pe, taken["exp"], 64, b, U * (g + 1))
                                for vector in (False, True):
                                    total = lo_count(vector, G * U)
                                    wait(pe, s_plo[vector], total, b, lo_count(vector, U * (g + 1)))
                            for j in range(GH):
                                h = g * GH + j
                                u = (j // 2) * 8 + kc * 2 + j % 2
                                o = OB[32 * j:32 * j + 32, :]
                                at = slice(h * VW, h * VW + 32)
                                if kc in SPLIT:
                                    v_hi, v_lo = (v_part(par, kc, k)[:, at] for k in range(2))
                                    terms = ((v_hi, p_part(u, 0)), (v_hi, p_part(u, 1)), (v_lo, p_part(u, 0)))
                                else:
                                    terms = ((v_aug[par][:, kc, at], probs[:, u, :]),)
                                for k, (st, mo) in enumerate(terms):
                                    ins = pe.matmul(o, st, mo, start=kc == 0 and k == 0,
                                                    stop=kc == TT - 1 and k == len(terms) - 1)
                            ins.then_inc(sig, 1)
                        elif kind == "h1T" or kind == "h2T" or kind == "onT":
                            if n == 0:
                                if kind == "h1T":
                                    wait(pe, s_ln1, 12, b, 12)
                                elif kind == "h2T":
                                    wait(pe, s_ln2, 12, b, 12)
                                else:
                                    wait(pe, taken["oT"], 4, b, 4)
                            for t in range(TT):
                                ins = pe.transpose(dst[:, t * P:(t + 1) * P], rows[:, t, n * P:(n + 1) * P], ident[:])
                            ins.then_inc(sig, 1)
                            if is_at(i, -1) and n == 1:
                                pe.wait_ge(s_w4s, 2)
                        elif kind == "oT":
                            if n == 0:
                                wait(pe, taken["pv"], 4, b, 4)
                            for g in range(G):
                                ins = pe.transpose(dst[:, g * P:(g + 1) * P], o_raw[:, g, n * P:(n + 1) * P], ident[:])
                            ins.then_inc(sig, 1)
                        elif kind == "qk":
                            if n == 0:
                                wait(pe, s_h1lo, 2, b, 2)
                            w, m = divmod(n, 2)
                            split_product(dst[:], [([p[:, w, c, m * P:(m + 1) * P] for p in w4],
                                                    [p[:, c, :] for p in h1]) for c in range(DC)]).then_inc(sig, 1)
                            if is_at(i, -1) and n == 3:
                                modulations(1)
                                modulations(2)
                        elif kind == "v" or kind == "wo":
                            a = h1 if kind == "v" else z
                            if n == 0 and kind == "wo":
                                wait(pe, s_onlo, 2, b, 2)
                            for t in range(2):
                                tok = (2 * n + t) * P
                                ins = split_product(dst[:, t * D:(t + 1) * D],
                                                    [([p[:, c, tok:tok + P] for p in a],
                                                      [p[:, 2 if kind == "v" else 3, c, :] for p in w4]) for c in range(DC)])
                            ins.then_inc(sig, 1)
                        elif kind == "logit":
                            wait(pe, s_h2lo, 2, b, 2)
                            for t in range(TT):
                                ins = split_product(dst[:, t * NR:(t + 1) * NR],
                                                    [([p[:, c, t * P:(t + 1) * P] for p in z],
                                                      [p[:, c, :] for p in wr]) for c in range(DC)])
                            ins.then_inc(sig, 1)
                        elif kind == "gateT":
                            wait(pe, s_top, 15, b, 15)
                            for t in range(TT):
                                ins = pe.transpose(dst[0:NR, t * P:(t + 1) * P], chosen[:, t, :], ident[:])
                            ins.then_inc(sig, 1)
                        elif kind == "up":
                            if n == 0:
                                pe.wait_ge(s_wlo, NW)
                            split_product(dst[:], [([p[:, c, n * E:(n + 1) * E] for p in wu],
                                                    [p[:, c, :] for p in z]) for c in range(DC)]).then_inc(sig, 1)
                        elif kind == "down":
                            c, t = divmod(n, TT)
                            if n == 0:
                                wait(pe, s_fin, 2, b, 0)
                            if t == 0:
                                wait(pe, s_elo, NEX, b, c + 1)
                            o = DB[t // 2][:, (t % 2) * D:(t % 2 + 1) * D]
                            for k, (a, w) in enumerate(((0, 0), (0, 1), (1, 0))):
                                ins = pe.matmul(o, act[a][:, c - SETS[SET_OF[c]], t * P:(t + 1) * P], wd[w][:, c, :],
                                                start=c == 0 and k == 0 and t % 2 == 0,
                                                stop=c == NEX - 1 and k == 2, skip_group_check=True)
                            ins.then_inc(sig, 1)

            iterations(pe, body)


def kernel(**inputs):
    import numpy as np
    import concourse.bacc as bacc
    from concourse import mybir as mb
    from concourse.bass_utils import run_bass_kernel_spmd as run

    a = {k[3:]: np.asarray(v) for k, v in inputs.items()}
    laid = {
        "x": a["attn_x"], "c_t": a["c"].T, "wmod": a["wmod"],
        "wqkvo": np.stack([a["attn_wq"], a["attn_wk"], a["attn_wv"], a["attn_wo"]]),
        "bqk": np.stack([a["attn_bq"], a["attn_bk"]]).reshape(4, P).T, "bv": a["attn_bv"], "bo": a["attn_bo"],
        "w_up": np.concatenate([a["ffn_shared_up"], a["ffn_routed_up"]]).reshape(NEX * E, D).T,
        "w_down": np.concatenate([a["ffn_shared_down"], a["ffn_routed_down"]]).transpose(2, 0, 1).reshape(E, NEX * D),
        "router": a["ffn_router_w"].T,
    }
    nc = bacc.Bacc("TRN2", target_bir_lowering=False, num_devices=1)
    arrays, args = {}, []
    for name, v in laid.items():
        v = np.ascontiguousarray(v)
        arrays[f"in_{name}"] = v
        args.append(nc.dram_tensor(f"in_{name}", v.shape, mb.dt.from_np(v.dtype), kind="ExternalInput").ap())
    out = nc.dram_tensor("out_0", (B, S, D), mb.dt.float32, kind="ExternalOutput").ap()
    block_kernel(nc, *args, out)
    r = run(nc, [arrays], core_ids=[0])
    return r.results[0]["out_0"]
```
